# Optimizing a Trainium2 kernel written in Bass

```python
import numpy as np
import jax
import jax.numpy as jnp

def _softmax(x, axis=-1):
    return jax.nn.softmax(x, axis=axis)

def _gelu(x):
    return jax.nn.gelu(x, approximate=True)

def _silu(x):
    return jax.nn.silu(x)

def _sigmoid(x):
    return jax.nn.sigmoid(x)

def _layernorm(x, axis=-1, eps=1e-05):
    m = jnp.mean(x, axis=axis, keepdims=True)
    v = jnp.var(x, axis=axis, keepdims=True)
    return (x - m) / jnp.sqrt(v + eps)

def _scatter_add(tgt, idx, src, axis=0):
    return tgt.at[idx].add(src)

def _segment_sum(src, seg, n):
    return jax.ops.segment_sum(src, seg, n)
kernel_name = 'mk_adj_resnorm_d1_adj_r2_83be5f'

def setup_inputs(seed: int=0):
    np.random.seed(seed)
    _w = jnp.asarray

    def _rec_inputs():
        import jax
        import jax.numpy as jnp
        _gk = jax.random.key(seed)
        x = -0.0005207 + 1.001 * jax.random.normal(jax.random.fold_in(_gk, 1), (4096, 256), jnp.float32)
        _a = jax.random.bernoulli(jax.random.fold_in(_gk, 2), 0.000488281, (4096, 4096))
        _af = _a.astype(jnp.float32)
        adj = _af
        return (x, adj)
    x, adj = _rec_inputs()

    def _L0_gnn_setup():
        import jax, jax.numpy as jnp
        import numpy as np
        N = 2048
        INPUT_DIM = 256
        KEY_DIM = 64
        OUT_DIM = 256
        N_HEADS = 8

        def _xavier_normal(key, shape, gain):
            fan_in, fan_out = (shape[-2], shape[-1])
            std = gain * (2.0 / (fan_in + fan_out)) ** 0.5
            return jax.random.normal(key, shape, dtype=jnp.float32) * std
        key = jax.random.key(seed)
        kx, ka, kk, kq, kv, ko = jax.random.split(key, 6)
        gain = 2.0 ** 0.5
        node_matrix = jax.random.normal(kx, (N, INPUT_DIM), dtype=jnp.float32)
        adjacency_matrix = jax.random.randint(ka, (N, N), 0, 2).astype(jnp.float32)
        Wks = _xavier_normal(kk, (N_HEADS, INPUT_DIM, KEY_DIM), gain)
        Wqs = _xavier_normal(kq, (N_HEADS, INPUT_DIM, KEY_DIM), gain)
        Wvs = _xavier_normal(kv, (N_HEADS, INPUT_DIM, KEY_DIM), gain)
        Wo = _xavier_normal(ko, (N_HEADS, KEY_DIM, OUT_DIM), gain)
        return {'node_matrix': node_matrix, 'adjacency_matrix': adjacency_matrix, 'Wks': Wks, 'Wqs': Wqs, 'Wvs': Wvs, 'Wo': Wo}
    _L0_gnn_all = _L0_gnn_setup()
    _L0_gnn_in = {k: v for k, v in _L0_gnn_all.items() if k in ('Wks', 'Wqs', 'Wvs', 'Wo')}
    del _L0_gnn_all
    return {'x': x, 'adj': adj, 'L0_gnn_Wks': _L0_gnn_in['Wks'], 'L0_gnn_Wqs': _L0_gnn_in['Wqs'], 'L0_gnn_Wvs': _L0_gnn_in['Wvs'], 'L0_gnn_Wo': _L0_gnn_in['Wo']}

def reference(x, adj, L0_gnn_Wks, L0_gnn_Wqs, L0_gnn_Wvs, L0_gnn_Wo):
    import jax
    import jax.numpy as jnp

    def _L0_gnn_ref(node_matrix, adjacency_matrix, Wks, Wqs, Wvs, Wo):
        import jax, jax.numpy as jnp
        import numpy as np
        N = 2048
        INPUT_DIM = 256
        KEY_DIM = 64
        OUT_DIM = 256
        N_HEADS = 8

        def _xavier_normal(key, shape, gain):
            fan_in, fan_out = (shape[-2], shape[-1])
            std = gain * (2.0 / (fan_in + fan_out)) ** 0.5
            return jax.random.normal(key, shape, dtype=jnp.float32) * std
        n = adjacency_matrix.shape[0]
        adj = jnp.maximum(adjacency_matrix, jnp.eye(n, dtype=adjacency_matrix.dtype))
        keys = jnp.einsum('nj,hjk->hnk', node_matrix, Wks)
        queries = jnp.einsum('nj,hjk->hnk', node_matrix, Wqs)
        values = jnp.einsum('nj,hjk->hnk', node_matrix, Wvs)
        key_dim = Wks.shape[-1]
        atts = jnp.einsum('hqk,hmk->hqm', queries, keys) / key_dim ** 0.5
        atts = atts - 1e+16 * (1.0 - adj)[None, :, :]
        atts = jax.nn.softmax(atts, axis=-1)
        return jnp.einsum('hqm,hmk,hko->qo', atts, values, Wo)
    x = _layernorm(x + _L0_gnn_ref(x, adj, L0_gnn_Wks, L0_gnn_Wqs, L0_gnn_Wvs, L0_gnn_Wo), axis=-1)
    return x

_drawn_inputs = setup_inputs


def setup_inputs(seed=0):
    import zlib

    import numpy as np

    out = dict(_drawn_inputs(seed))
    spreads = {}
    factors = {}
    for name, (base, spread) in spreads.items():
        noise = np.random.default_rng([zlib.crc32(name.encode()), seed]).standard_normal(out[name].shape)
        drawn = base * np.exp(spread * noise) if base else spread * noise
        out[name] = jnp.asarray(drawn.astype(out[name].dtype))
    for name, factor in factors.items():
        out[name] = (out[name] * factor).astype(out[name].dtype)
    return out
```

```python
import concourse.bass as bass
from concourse import mybir
from contextlib import ExitStack


def graph_attention_resnorm_kernel(nc, x, adj, wks, wqs, wvs, wo, out):
    fp32 = mybir.dt.float32
    ALU = mybir.AluOpType
    ACT = mybir.ActivationFunctionType
    AX = mybir.AxisListType

    P = 128
    N, D = x.shape
    H, _, KD = wks.shape
    HK = H * KD
    T = N // P
    DC = D // P
    EPS = 1e-5
    BIG = 1e16
    SCALE = float(KD) ** -0.5
    BANK = 512
    NB = N // BANK

    kv = nc.dram_tensor("kv_table", (N, 2 * HK), fp32, kind="Internal").ap()
    qx = nc.dram_tensor("qx_table", (N, HK + D), fp32, kind="Internal").ap()

    ctx = ExitStack()
    with ctx:
        def sb(name, shape, dt=fp32):
            return ctx.enter_context(nc.sbuf_tensor(name, shape, dt))

        def pb(name, shape, dt=fp32):
            return ctx.enter_context(nc.psum_tensor(name, shape, dt))

        def sem(name):
            return ctx.enter_context(nc.semaphore(name))

        ident = sb("ident", [P, P])
        w = sb("w", [P, DC, 3 * HK])
        xT = sb("xT", [P, 2, DC, P])
        row = sb("row", [P, 2, 3 * HK + D])
        logits = sb("logits", [P, N])
        kT = sb("kT", [KD, N])
        vh = sb("vh", [P, T, KD])
        woh = sb("woh", [KD, D])
        k_nat = sb("k_nat", [P, 4, KD])
        q_nat = sb("q_nat", [P, KD])
        qT = sb("qT", [KD, P])
        pT = sb("pT", [P, 2, BANK])
        res = sb("res", [P, T, D])
        o_n = sb("o_n", [P, KD])
        oT = sb("oT", [KD, P])
        nmax = sb("nmax", [P, 1])
        rsum = sb("rsum", [P, 1])
        rinv = sb("rinv", [P, 1])
        stats = sb("stats", [P, 6])
        mv = sb("mv", [P, 2])
        eps = sb("eps", [P, 1])
        std = sb("std", [P, 1])
        rstd = sb("rstd", [P, 1])

        banks = [pb(f"bank{i}", [P, BANK]) for i in range(8)]

        w_in = sem("w_in")
        ident_zero = sem("ident_zero")
        ident_ok = sem("ident_ok")
        xT_ps = sem("xT_ps")
        xT_ok = sem("xT_ok")
        kvq_ps = sem("kvq_ps")
        kvq_copied_a = sem("kvq_copied_a")
        kvq_copied_v = sem("kvq_copied_v")
        g_res_in = sem("g_res_in")
        g_head_in = sem("g_head_in")
        g_k_in = sem("g_k_in")
        g_kT_ps = sem("g_kT_ps")
        g_kT_ok = sem("g_kT_ok")
        g_q_in = sem("g_q_in")
        g_adj_in = sem("g_adj_in")
        g_qT_ps = sem("g_qT_ps")
        g_qT_ok = sem("g_qT_ok")
        g_diag = sem("g_diag")
        g_bias = sem("g_bias")
        g_s_ps = sem("g_s_ps")
        g_logits = sem("g_logits")
        g_max = sem("g_max")
        g_exp = sem("g_exp")
        g_rinv = sem("g_rinv")
        g_pT_ps = sem("g_pT_ps")
        g_pT_ok = sem("g_pT_ok")
        g_pv = sem("g_pv")
        g_o = sem("g_o")
        g_oT_ps = sem("g_oT_ps")
        g_oT_ok = sem("g_oT_ok")
        g_head_done = sem("g_head_done")
        g_res = sem("g_res")
        g_stats = sem("g_stats")
        g_mv = sem("g_mv")
        g_std = sem("g_std")
        g_rstd = sem("g_rstd")
        g_ln = sem("g_ln")
        g_eps = sem("g_eps")
        g_out = sem("g_out")
        passed_dve = sem("passed_dve")
        passed_pe = sem("passed_pe")
        passed_sp = sem("passed_sp")
        x_in = [sem(f"x_in{i}") for i in range(2)]
        rows_out = [sem(f"rows_out{i}") for i in range(2)]

        block = ctx.enter_context(nc.Block())

        x_v = x.rearrange("(t p) d -> t p d", p=P)
        kv_v = kv.rearrange("(t p) c -> t p c", p=P)
        qx_v = qx.rearrange("(t p) c -> t p c", p=P)
        kv_h = kv.rearrange("(t p) (g k) -> p t g k", p=P, k=KD)
        kv_b = kv.rearrange("(b t p) (g k) -> b p t g k", p=P, t=4, k=KD)
        qx_t = qx.rearrange("(t p) (g k) -> t p g k", p=P, k=KD)
        adj_t = adj.rearrange("(t p) m -> t p m", p=P)
        out_t = out.rearrange("(t p) d -> t p d", p=P)

        @block.sync
        def _(sp):
            for c in range(DC):
                for j, wsrc in enumerate((wks, wvs, wqs)):
                    sp.dma_start(w[:, c, j * HK:(j + 1) * HK].rearrange("p (h k) -> p h k", h=H),
                                 wsrc[:, c * P:(c + 1) * P, :].rearrange("h p k -> p h k")).then_inc(w_in, 16)

            for s in range(2):
                sp.dma_start(row[:, s, 3 * HK:], x_v[s, :, :]).then_inc(x_in[s], 16)
            with sp.Fori(0, T // 2) as i:
                for s in range(2):
                    t = i * 2 + s
                    sp.wait_ge(kvq_copied_a, t * 2 + 2)
                    sp.sem_inc(passed_sp, 1)
                    sp.wait_ge(kvq_copied_v, t + 1)
                    sp.sem_inc(passed_sp, 1)
                    sp.dma_start(kv_v[t, :, :], row[:, s, 0:2 * HK]).then_inc(rows_out[s], 16)
                    sp.dma_start(qx_v[t, :, :], row[:, s, 2 * HK:]).then_inc(rows_out[s], 16)
                    sp.wait_ge(rows_out[s], i * 32 + 32)
                    sp.dma_start(row[:, s, 3 * HK:], x_v[(t + 2) % T, :, :]).then_inc(x_in[s], 16)
            for s in range(2):
                sp.wait_ge(x_in[s], 16 * (T // 2 + 1))

            sp.dma_start(res[:], x.rearrange("(t p) d -> p t d", p=P)).then_inc(g_res_in, 16)
            with sp.Fori(0, H) as h:
                sp.wait_ge(g_head_done, h * T + 1)
                sp.dma_start(vh[:], kv_h[:, :, H + h, :]).then_inc(g_head_in, 16)
                sp.dma_start(woh[:], wo[h, :, :]).then_inc(g_head_in, 16)
                with sp.Fori(0, NB) as b:
                    sp.wait_ge(g_kT_ps, h * NB + b + 1)
                    sp.dma_start(k_nat[:], kv_b[b, :, :, h, :]).then_inc(g_k_in, 16)
                with sp.Fori(0, T) as t:
                    sp.wait_ge(g_qT_ps, h * T + t + 1)
                    sp.dma_start(q_nat[:], qx_t[t, :, h, :]).then_inc(g_q_in, 16)
                    sp.wait_ge(g_pT_ps, (h * T + t) * NB + 1)
                    sp.dma_start(logits[:], adj_t[t, :, :]).then_inc(g_adj_in, 16)
            with sp.Fori(0, T) as t:
                sp.wait_ge(g_ln, t + 1)
                sp.dma_start(out_t[t, :, :], res[:, t, :]).then_inc(g_out, 16)
            sp.wait_ge(g_out, 16 * T)

        @block.gpsimd
        def _(pool):
            nc.gpsimd.memset(ident[:], 0.0).then_inc(ident_zero, 1)
            pool.wait_ge(ident_zero, 1)
            nc.gpsimd.affine_select(out=ident[:], in_=ident[:], compare_op=ALU.not_equal, fill=1.0, base=0,
                                    pattern=[[-1, P]], channel_multiplier=1).then_inc(ident_ok, 1)

        @block.tensor
        def _(pe):
            pe.wait_ge(ident_ok, 1)
            pe.wait_ge(w_in, 16 * 3 * DC)
            def row_pair(i, first=False):
                for s in range(2):
                    t = i * 2 + s
                    pe.wait_ge(x_in[s], i * 16 + 16)
                    for c in range(DC):
                        last = nc.tensor.transpose(banks[s][:, c * P:(c + 1) * P],
                                                   row[:, s, 3 * HK + c * P:3 * HK + (c + 1) * P], ident[:])
                    last.then_inc(xT_ps, 1)
                    pe.wait_ge(xT_ok, t + 1)
                    if not first:
                        pe.wait_ge(kvq_copied_a, t * 2 - 2)
                        pe.wait_ge(kvq_copied_v, t - 1)
                    for j in range(3):
                        for c in range(DC):
                            last = nc.tensor.matmul(banks[2 + 3 * s + j][:], xT[:, s, c, :], w[:, c, j * HK:(j + 1) * HK],
                                                    start=(c == 0), stop=(c == DC - 1))
                        last.then_inc(kvq_ps, 1)

            row_pair(0, first=True)
            with pe.Fori(1, T // 2) as i:
                row_pair(i)

            for count in (g_head_done, g_kT_ps, g_qT_ps, g_pT_ps, g_pv, g_s_ps):
                pe.sem_inc(count, 1)
            with pe.Fori(0, H) as h:
                with pe.Fori(0, NB) as b:
                    pe.wait_ge(g_k_in, (h * NB + b + 1) * 16)
                    pe.wait_ge(g_kT_ok, h * NB + b + 1)
                    pe.sem_inc(passed_pe, 1)
                    for j in range(4):
                        last = nc.tensor.transpose(banks[0][0:KD, j * P:(j + 1) * P], k_nat[:, j, :], ident[:])
                    last.then_inc(g_kT_ps, 1)
                pe.wait_ge(g_kT_ok, (h + 1) * NB + 1)
                pe.wait_ge(g_head_in, (h + 1) * 32)
                pe.sem_inc(passed_pe, 1)
                with pe.Fori(0, T) as t:
                    n = h * T + t
                    pe.wait_ge(g_q_in, (n + 1) * 16)
                    pe.sem_inc(passed_pe, 1)
                    nc.tensor.transpose(banks[1][0:KD, 0:P], q_nat[:], ident[:]).then_inc(g_qT_ps, 1)
                    pe.wait_ge(g_qT_ok, n + 1)
                    for c in range(NB):
                        if c < 2:
                            pe.wait_ge(g_logits, n * NB + 1)
                        else:
                            pe.wait_ge(g_logits, n * NB + c - 1 + 1)
                        nc.tensor.matmul(banks[2 + c % 2][:], qT[:], kT[:, c * BANK:(c + 1) * BANK],
                                         start=True, stop=True).then_inc(g_s_ps, 1)
                    pe.wait_ge(g_exp, n + 1)
                    pe.wait_ge(g_o, n + 1)
                    for c in range(NB):
                        if c < 2:
                            pe.wait_ge(g_pT_ok, n * NB + 1)
                        else:
                            pe.wait_ge(g_pT_ok, n * NB + c - 1 + 1)
                        for j in range(4):
                            last = nc.tensor.transpose(banks[4 + c % 2][:, j * P:(j + 1) * P],
                                                       logits[:, (4 * c + j) * P:(4 * c + j + 1) * P], ident[:])
                        last.then_inc(g_pT_ps, 1)
                        pe.wait_ge(g_pT_ok, n * NB + c + 1 + 1)
                        for j in range(4):
                            last = nc.tensor.matmul(banks[6][:, 0:KD], pT[:, c % 2, j * P:(j + 1) * P], vh[:, 4 * c + j, :],
                                                    start=(c + j == 0), stop=(c == NB - 1 and j == 3))
                        last.then_inc(g_pv, 1)
                    pe.wait_ge(g_o, n + 1 + 1)
                    pe.sem_inc(passed_pe, 1)
                    nc.tensor.transpose(banks[1][0:KD, 0:P], o_n[:], ident[:]).then_inc(g_oT_ps, 1)
                    pe.wait_ge(g_oT_ok, n + 1)
                    pe.wait_ge(g_res, n + 1)
                    nc.tensor.matmul(banks[7][:, 0:D], oT[:], woh[:], start=True, stop=True).then_inc(g_head_done, 1)

        @block.scalar
        def _(act):
            def row_pair(i, first=False):
                for s in range(2):
                    t = i * 2 + s
                    act.wait_ge(xT_ps, t + 1)
                    if not first:
                        act.wait_ge(kvq_ps, t * 3 - 3)
                    nc.scalar.copy(xT[:, s, :, :], banks[s][:, 0:D].rearrange("p (c q) -> p c q", c=DC)).then_inc(xT_ok, 1)
                    if not first:
                        act.wait_ge(rows_out[s], i * 32)
                    for j in range(2):
                        act.wait_ge(kvq_ps, t * 3 + j + 1)
                        nc.scalar.copy(row[:, s, j * HK:(j + 1) * HK], banks[2 + 3 * s + j][:]).then_inc(kvq_copied_a, 1)

            row_pair(0, first=True)
            with act.Fori(1, T // 2) as i:
                row_pair(i)

            for count in (g_kT_ok, g_pT_ok):
                act.sem_inc(count, 1)
            with act.Fori(0, H) as h:
                with act.Fori(0, NB) as b:
                    act.wait_ge(g_kT_ps, h * NB + b + 1 + 1)
                    act.wait_ge(g_head_done, h * T + 1)
                    nc.scalar.copy(kT[:, bass.ds(b * BANK, BANK)], banks[0][0:KD, :]).then_inc(g_kT_ok, 1)
                with act.Fori(0, T) as t:
                    n = h * T + t
                    act.wait_ge(g_qT_ps, n + 1 + 1)
                    act.wait_ge(g_s_ps, n * NB + 1)
                    nc.scalar.copy(qT[:], banks[1][0:KD, 0:P]).then_inc(g_qT_ok, 1)
                    act.wait_ge(g_max, n + 1)
                    nc.scalar.activation(logits[:], logits[:], ACT.Exp, bias=nmax[:, 0:1],
                                         accum_out=rsum[:, 0:1]).then_inc(g_exp, 1)
                    for c in range(NB):
                        act.wait_ge(g_pT_ps, n * NB + c + 1 + 1)
                        if c < 2:
                            act.wait_ge(g_pv, n * NB + 1)
                        else:
                            act.wait_ge(g_pv, n * NB + c - 1 + 1)
                        nc.scalar.copy(pT[:, c % 2, :], banks[4 + c % 2][:]).then_inc(g_pT_ok, 1)
                    act.wait_ge(g_oT_ps, n + 1)
                    nc.scalar.copy(oT[:], banks[1][0:KD, 0:P]).then_inc(g_oT_ok, 1)
            act.wait_ge(g_eps, 1)
            with act.Fori(0, T) as t:
                act.wait_ge(g_mv, t + 1)
                nc.scalar.activation(std[:], mv[:, 1:2], ACT.Sqrt, bias=eps[:, 0:1]).then_inc(g_std, 1)

        @block.vector
        def _(dve):
            nc.vector.memset(eps[:], EPS).then_inc(g_eps, 1)
            def row_pair(i, first=False):
                for s in range(2):
                    t = i * 2 + s
                    if not first:
                        dve.wait_ge(rows_out[s], i * 32)
                    dve.wait_ge(kvq_ps, t * 3 + 3)
                    nc.vector.tensor_copy(row[:, s, 2 * HK:3 * HK], banks[2 + 3 * s + 2][:]).then_inc(kvq_copied_v, 1)

            row_pair(0, first=True)
            with dve.Fori(1, T // 2) as i:
                row_pair(i)

            for count in (g_logits, g_o, g_res):
                dve.sem_inc(count, 1)
            dve.wait_ge(g_res_in, 16)
            with dve.Fori(0, H) as h:
                with dve.Fori(0, T) as t:
                    n = h * T + t
                    dve.wait_ge(g_adj_in, (n + 1) * 16)
                    nc.vector.tensor_tensor(logits[:, bass.ds(t * P, P)], logits[:, bass.ds(t * P, P)], ident[:],
                                            ALU.max).then_inc(g_diag, 1)
                    dve.wait_ge(g_diag, n + 1)
                    nc.vector.tensor_scalar(logits[:], logits[:], -1.0, BIG, ALU.add, ALU.mult).then_inc(g_bias, 1)
                    dve.wait_ge(g_bias, n + 1)
                    for c in range(NB):
                        dve.wait_ge(g_s_ps, n * NB + c + 1 + 1)
                        piece = logits[:, c * BANK:(c + 1) * BANK]
                        nc.vector.scalar_tensor_tensor(out=piece, in0=banks[2 + c % 2][:], scalar=SCALE, in1=piece,
                                                       op0=ALU.mult, op1=ALU.add).then_inc(g_logits, 1)
                    dve.wait_ge(g_logits, (n + 1) * NB + 1)
                    nc.vector.tensor_reduce(nmax[:], logits[:], AX.X, ALU.max, negate=True).then_inc(g_max, 1)
                    dve.wait_ge(g_exp, n + 1)
                    nc.vector.reciprocal(rinv[:], rsum[:]).then_inc(g_rinv, 1)
                    dve.wait_ge(g_rinv, n + 1)
                    dve.wait_ge(g_pv, (n + 1) * NB + 1)
                    nc.vector.tensor_scalar(o_n[:], banks[6][:, 0:KD], rinv[:, 0:1], None, ALU.mult).then_inc(g_o, 1)
                    dve.wait_ge(g_head_done, n + 1 + 1)
                    r = res[:, bass.ds(t, 1), :].rearrange("p a d -> p (a d)")
                    nc.vector.tensor_tensor(r, r, banks[7][:, 0:D], ALU.add).then_inc(g_res, 1)
            dve.wait_ge(g_res, H * T + 1)
            with dve.Fori(0, T) as t:
                r = res[:, bass.ds(t, 1), :].rearrange("p a d -> p (a d)")
                nc.vector.bn_stats(stats[:], r).then_inc(g_stats, 1)
                dve.wait_ge(g_stats, t + 1)
                dve.sem_inc(passed_dve, 1)
                nc.vector.bn_aggr(mv[:], stats[:]).then_inc(g_mv, 1)
                dve.wait_ge(g_std, t + 1)
                nc.vector.reciprocal(rstd[:], std[:]).then_inc(g_rstd, 1)
                dve.wait_ge(g_rstd, t + 1)
                dve.wait_ge(g_mv, t + 1)
                nc.vector.tensor_scalar(r, r, mv[:, 0:1], rstd[:, 0:1], ALU.subtract, ALU.mult).then_inc(g_ln, 1)


_INS = ['x', 'adj', 'L0_gnn_Wks', 'L0_gnn_Wqs', 'L0_gnn_Wvs', 'L0_gnn_Wo']


def kernel(**inputs):
    import numpy as _np
    import concourse.bacc as _bacc
    from concourse import mybir as _mybir
    from concourse.bass_utils import run_bass_kernel_spmd as _run

    nc = _bacc.Bacc("TRN2", target_bir_lowering=False, num_devices=1)
    arrays, args = {}, []
    for name in _INS:
        a = _np.ascontiguousarray(inputs[name])
        arrays[f"in_{name}_dram"] = a
        args.append(nc.dram_tensor(f"in_{name}_dram", a.shape, _mybir.dt.from_np(a.dtype), kind="ExternalInput").ap())
    shape = inputs['x'].shape
    args.append(nc.dram_tensor("out_0_dram", shape, _mybir.dt.float32, kind="ExternalOutput").ap())
    graph_attention_resnorm_kernel(nc, *args)
    r = _run(nc, [arrays], core_ids=[0])
    return r.results[0]["out_0_dram"]
```

```python
import concourse.bass as bass
from concourse import mybir
from contextlib import ExitStack


def graph_attention_resnorm_kernel(nc, x, adj, wks, wqs, wvs, wo, out):
    fp32 = mybir.dt.float32
    bf16 = mybir.dt.bfloat16
    i32 = mybir.dt.int32
    u32 = mybir.dt.uint32
    ALU = mybir.AluOpType
    ACT = mybir.ActivationFunctionType
    AX = mybir.AxisListType

    P = 128
    N, D = x.shape
    H, _, KD = wks.shape
    HK = H * KD
    T = N // P
    DC = D // P
    HC = HK // P
    EPS = 1e-5
    BIG = 1e16
    SCALE = float(KD) ** -0.5
    BANK = 512
    NB = N // BANK

    DIGITS = N // BANK
    KEY = BANK
    SEGS = 4
    SEG = BANK // SEGS
    LEVELS = 3
    BIAS = 127 * KEY
    NEAR = 16
    CAND = LEVELS * SEGS * 8
    SIDES = 4
    WIDE = 6
    FIRST = 2 * WIDE
    QUADS = [(0, 1, WIDE), (1, 1, 5), (2, 1, 4), (3, 2, 3), (5, 3, 2)]

    LIMITS = [(0, 1, FIRST), (1, 4, WIDE)] + [(4 * q, 4 * (q + n), c) for q, n, c in QUADS[1:]]
    NBAD = T // 2 + len(LIMITS)
    STEPS = 4 + 4 * LEVELS + 1 + 12 + 3

    kv = nc.dram_tensor("kv_table", (N, 2 * HK), fp32, kind="Internal").ap()
    qx = nc.dram_tensor("qx_table", (N, HK + D), fp32, kind="Internal").ap()
    order = nc.dram_tensor("order_table", (N, 1 + NEAR), i32, kind="Internal").ap()

    ctx = ExitStack()
    with ctx:
        def sb(name, shape, dt=fp32):
            return ctx.enter_context(nc.sbuf_tensor(name, shape, dt))

        def sem(name):
            return ctx.enter_context(nc.semaphore(name))

        ident = sb("ident", [P, P])
        digit = sb("digit", [P, DIGITS, P], bf16)
        column = sb("column", [2, BANK], bf16)
        column_lo = sb("column_lo", [1, BANK], bf16)
        ones2 = sb("ones2", [2, P], bf16)
        ones = sb("ones", [P, P], bf16)
        before = sb("before", [P, P], bf16)
        ones_f = sb("ones_f", [P, BANK])
        degrees = sb("degrees", [P, NEAR, T])
        w = sb("w", [P, DC, 3 * HK])
        wo_sb = sb("wo_sb", [P, HC, D])
        row = sb("row", [P, SIDES, 3 * HK + D])
        arena = sb("arena", [P, SIDES * WIDE, 2 * HK])
        adj_sb = arena[:, 0:4 * SIDES, :].rearrange("p (s a) c -> p s (a c)", s=SIDES)
        xT = sb("xT", [P, 2, DC, P])
        keys = sb("keys", [P, 4, SEGS * 8], i32)
        col = sb("col", [P, 4, SEGS * 8], i32)
        bits = sb("bits", [P, 4, SEGS * 8], i32)
        val = sb("val", [P, LEVELS + 1, 4, SEGS * 8])
        expo = sb("expo", [P, 4, SEGS * 8], i32)
        power = sb("power", [P, 4, SEGS * 8], i32)
        cand = sb("cand", [P, 4, CAND])
        cand2 = sb("cand2", [P, 4, CAND])
        top = sb("top", [P, 4, NEAR])
        rec = sb("rec", [P, T, 1 + NEAR], i32)
        listed = sb("listed", [P, 4, NEAR])
        degree = sb("degree", [P, T])
        onehot = sb("onehot", [P, NEAR, T], bf16)
        place = sb("place", [P, NEAR, T])
        rank = sb("rank", [P, T], i32)
        srt = sb("srt", [P, T, 1 + NEAR], i32)
        near = sb("near", [P, T, 1 + NEAR], i32)
        mask = sb("mask", [P, T, NEAR])
        near_q = sb("near_q", [P, SIDES, 1 + NEAR], i32)
        out_q = sb("out_q", [P, SIDES, 1], i32)
        crowd = sb("crowd", [P, T // 2])
        excess = sb("excess", [P, len(LIMITS)])
        bad = sb("bad", [P, NBAD])
        flag = sb("flag", [P, 1], i32)
        lg = sb("lg", [P, SIDES, FIRST, H])
        pr = sb("pr", [P, SIDES, FIRST, H])
        mx = sb("mx", [P, SIDES, H])
        sm = sb("sm", [P, SIDES, H])
        inv = sb("inv", [P, SIDES, H])
        o_sb = sb("o_sb", [P, HK])
        oT_sb = sb("oT_sb", [P, HC, P])
        joined_sb = sb("joined_sb", [P, SIDES, D])
        st = sb("st", [P, SIDES, 6])
        mv4 = sb("mv4", [P, SIDES, 2])
        lnv = sb("lnv", [P, SIDES, 1])
        rs4 = sb("rs4", [P, SIDES, 1])
        eps = sb("eps", [P, 1])
        logits = adj_sb[:, 0, :]
        kT = adj_sb[0:KD, 1, :]
        vh = adj_sb[:, 2, 0:T * KD].rearrange("p (t k) -> p t k", k=KD)
        res = arena[:, 4 * SIDES:, :].rearrange("p a c -> p (a c)")[:, 0:T * D].rearrange("p (t d) -> p t d", d=D)
        woh = sb("woh", [KD, D])
        k_nat = sb("k_nat", [P, 4, KD])
        q_nat = sb("q_nat", [P, KD])
        qT = sb("qT", [KD, P])
        pT = sb("pT", [P, 2, BANK])
        o_n = sb("o_n", [P, KD])
        oT = sb("oT", [KD, P])
        nmax = sb("nmax", [P, 1])
        rsum = sb("rsum", [P, 1])
        rinv = sb("rinv", [P, 1])
        stats = sb("stats", [P, 6])
        mv = sb("mv", [P, 2])
        std = sb("std", [P, 1])
        rstd = sb("rstd", [P, 1])

        banks = [ctx.enter_context(nc.psum_tensor(f"bank{i}", [P, BANK], fp32)) for i in range(8)]
        PACK, XT, KVQ = 0, 2, 4
        O_PS, OT_PS, Y_PS = 0, 2, 3

        column_ok = sem("column_ok")
        column_in = sem("column_in")
        w_in = sem("w_in")
        packed = sem("packed")
        kv_copied = sem("kv_copied")
        q_copied = sem("q_copied")
        wo_in = sem("wo_in")
        order_out = sem("order_out")
        order_in = sem("order_in")
        flag_ok = sem("flag_ok")
        sparse_done = sem("sparse_done")
        ident_zero = sem("ident_zero")
        ident_ok = sem("ident_ok")
        before_zero = sem("before_zero")
        sort_consts = sem("sort_consts")
        rec_rows = sem("rec_rows")
        diag_ok = sem("diag_ok")
        rank_ok = sem("rank_ok")
        near_ok = sem("near_ok")
        pv_ps = sem("pv_ps")
        joined = sem("joined")
        near_copied = sem("near_copied")
        normed = sem("normed")
        outq_copied = sem("outq_copied")
        digits_ok = sem("digits_ok")
        keys_ok = sem("keys_ok")
        xT_ps = sem("xT_ps")
        xT_ok = sem("xT_ok")
        kvq_ps = sem("kvq_ps")
        onehot_ok = sem("onehot_ok")
        place_ps = sem("place_ps")
        bad_ok = sem("bad_ok")
        bad_ps = sem("bad_ps")
        weighted = sem("weighted")
        o_copied = sem("o_copied")
        oT_ps = sem("oT_ps")
        oT_copied = sem("oT_copied")
        y_ps = sem("y_ps")
        eps_ok = sem("eps_ok")
        shifted = sem("shifted")
        exps = sem("exps")
        moments = sem("moments")
        ln_ok = sem("ln_ok")
        rs_ok = sem("rs_ok")
        dve_chain = sem("dve_chain")
        decoded = sem("decoded")
        products = sem("products")
        scores = sem("scores")
        masked = sem("masked")
        maxima = sem("maxima")
        sums = sem("sums")
        inverses = sem("inverses")
        probs = sem("probs")
        half_moments = sem("half_moments")
        adj_in = [sem(f"adj_in{i}") for i in range(SIDES)]
        given = [sem(f"given{i}") for i in range(SIDES)]
        kv_in = [sem(f"kv_in{i}") for i in range(SIDES)]
        qx_in = [sem(f"qx_in{i}") for i in range(SIDES)]
        rows_out = [sem(f"rows_out{i}") for i in range(SIDES)]
        x_in = [sem(f"x_in{i}") for i in range(SIDES)]
        passed_sp = sem("passed_sp")
        passed_pe = sem("passed_pe")
        passed_dve = sem("passed_dve")
        passed_pool = sem("passed_pool")
        g_res_in = sem("g_res_in")
        g_head_in = sem("g_head_in")
        g_k_in = sem("g_k_in")
        g_kT_ps = sem("g_kT_ps")
        g_kT_ok = sem("g_kT_ok")
        g_q_in = sem("g_q_in")
        g_adj_in = sem("g_adj_in")
        g_qT_ps = sem("g_qT_ps")
        g_qT_ok = sem("g_qT_ok")
        g_diag = sem("g_diag")
        g_bias = sem("g_bias")
        g_s_ps = sem("g_s_ps")
        g_logits = sem("g_logits")
        g_max = sem("g_max")
        g_exp = sem("g_exp")
        g_rinv = sem("g_rinv")
        g_pT_ps = sem("g_pT_ps")
        g_pT_ok = sem("g_pT_ok")
        g_pv = sem("g_pv")
        g_o = sem("g_o")
        g_oT_ps = sem("g_oT_ps")
        g_oT_ok = sem("g_oT_ok")
        g_head_done = sem("g_head_done")
        g_res = sem("g_res")
        g_stats = sem("g_stats")
        g_mv = sem("g_mv")
        g_std = sem("g_std")
        g_rstd = sem("g_rstd")
        g_ln = sem("g_ln")
        g_out = sem("g_out")

        block = ctx.enter_context(nc.Block())

        x_v = x.rearrange("(t p) d -> t p d", p=P)
        adj_t = adj.rearrange("(t p) m -> t p m", p=P)
        kv_v = kv.rearrange("(t p) c -> t p c", p=P)
        qx_v = qx.rearrange("(t p) c -> t p c", p=P)
        kv_h = kv.rearrange("(t p) (g k) -> p t g k", p=P, k=KD)
        kv_b = kv.rearrange("(b t p) (g k) -> b p t g k", p=P, t=4, k=KD)
        qx_t = qx.rearrange("(t p) (g k) -> t p g k", p=P, k=KD)
        out_t = out.rearrange("(t p) d -> t p d", p=P)

        def side_of(u):
            return (u + 3) % SIDES

        def gathered(u, c, first):
            at = 2 * WIDE if first else side_of(u) * WIDE
            return arena[:, at:at + c, :]

        def turns(quads):
            before_them = [0] * SIDES
            for q0, nq, c in quads:
                for k0, nk in ((q0, 1),) if q0 == 0 else ((q0, nq),):
                    cs = [FIRST if q0 == 0 and u == 0 else c for u in range(4)]
                    yield k0, nk, cs, list(before_them)
                    for u in range(4):
                        before_them[side_of(u)] += nk * cs[u]

        TURNS = list(turns(QUADS))
        assert TURNS[-1][0] + TURNS[-1][1] == T // 4

        @block.sync
        def _(sp):
            sp.wait_ge(column_ok, 2)
            sp.dma_start(column[1:2, :], column_lo[0:1, :]).then_inc(column_in, 16)
            for s in range(2):
                sp.dma_start(row[:, s, 3 * HK:], x_v[s, :, :]).then_inc(x_in[s], 16)
            for c in range(DC):
                for j, wsrc in enumerate((wks, wvs, wqs)):
                    sp.dma_start(w[:, c, j * HK:(j + 1) * HK].rearrange("p (h k) -> p h k", h=H),
                                 wsrc[:, c * P:(c + 1) * P, :].rearrange("h p k -> p h k")).then_inc(w_in, 16)

            def step(i, s, first=False, last=False):
                t = i * 4 + s
                if not first:
                    sp.wait_ge(packed, t - 3)
                sp.dma_start(adj_sb[:, s, :], adj_t[t, :, :]).then_inc(adj_in[s], 16)
                if not first or s >= 2:
                    store(i, s, first)
                if first and s == 0 or last and s == 3:
                    return
                n = (s + 1) % 4
                if not first or s == 3:
                    sp.wait_ge(rows_out[n], (i + (s == 3)) * 32)
                sp.dma_start(row[:, n, 3 * HK:], x_v[t + 1, :, :]).then_inc(x_in[n], 16)

            def store(i, s, first=False):
                t = i * 4 + s
                b = (s + 2) % 4
                sp.wait_ge(kv_copied, t * 2 - 2)
                sp.sem_inc(passed_sp, 1)
                sp.wait_ge(q_copied, t - 1)
                sp.sem_inc(passed_sp, 1)
                sp.dma_start(kv_v[t - 2, :, :], row[:, b, 0:2 * HK]).then_inc(rows_out[b], 16)
                sp.dma_start(qx_v[t - 2, :, :], row[:, b, 2 * HK:]).then_inc(rows_out[b], 16)

            for s in range(4):
                step(0, s, first=True)
            with sp.Fori(1, T // 4 - 1) as i:
                for s in range(4):
                    step(i, s)
            for s in range(4):
                step(T // 4 - 1, s, last=True)
            for s in range(2):
                store(T // 4, s)
            sp.dma_start(wo_sb[:], wo.rearrange("h k o -> (h k) o").rearrange("(c p) o -> p c o", p=P)).then_inc(wo_in, 16)
            sp.wait_ge(order_out, 16 * T)
            sp.dma_start(srt[:], order.rearrange("(i p) c -> p i c", p=P)).then_inc(order_in, 16)

            sp.wait_ge(flag_ok, 1)
            crowded = sp.value_load(flag[0:1, 0:1], min_val=0, max_val=1 << 20)
            sp.wait_ge(sparse_done, 1)
            with sp.If(crowded > 0):
                sp.dma_start(res[:], x.rearrange("(t p) d -> p t d", p=P)).then_inc(g_res_in, 16)
                with sp.Fori(0, H) as h:
                    sp.wait_ge(g_head_done, h * T + 1)
                    sp.dma_start(vh[:], kv_h[:, :, H + h, :]).then_inc(g_head_in, 16)
                    sp.dma_start(woh[:], wo[h, :, :]).then_inc(g_head_in, 16)
                    with sp.Fori(0, NB) as b:
                        sp.wait_ge(g_kT_ps, h * NB + b + 1)
                        sp.dma_start(k_nat[:], kv_b[b, :, :, h, :]).then_inc(g_k_in, 16)
                    with sp.Fori(0, T) as t:
                        sp.wait_ge(g_qT_ps, h * T + t + 1)
                        sp.dma_start(q_nat[:], qx_t[t, :, h, :]).then_inc(g_q_in, 16)
                        sp.wait_ge(g_pT_ps, (h * T + t) * NB + 1)
                        sp.dma_start(logits[:], adj_t[t, :, :]).then_inc(g_adj_in, 16)
                with sp.Fori(0, T) as t:
                    sp.wait_ge(g_ln, t + 1)
                    sp.dma_start(out_t[t, :, :], res[:, t, :]).then_inc(g_out, 16)
                sp.wait_ge(g_out, 16 * T)

        @block.gpsimd
        def _(pool):
            nc.gpsimd.memset(ident[:], 0.0).then_inc(ident_zero, 1)
            nc.gpsimd.iota(column[0:1, :], [[256, BANK // 256], [0, 256]], base=0, channel_multiplier=0,
                           allow_small_or_imprecise_dtypes=True).then_inc(column_ok, 1)
            nc.gpsimd.iota(column_lo[:], [[0, BANK // 256], [1, 256]], base=0, channel_multiplier=0,
                           allow_small_or_imprecise_dtypes=True).then_inc(column_ok, 1)
            pool.wait_ge(ident_zero, 1)
            nc.gpsimd.affine_select(out=ident[:], in_=ident[:], compare_op=ALU.not_equal, fill=1.0, base=0,
                                    pattern=[[-1, P]], channel_multiplier=1).then_inc(ident_ok, 1)
            nc.gpsimd.memset(before[:], 0.0).then_inc(before_zero, 1)
            nc.gpsimd.memset(ones[:], 1.0).then_inc(sort_consts, 1)
            nc.gpsimd.iota(degrees[:], [[-1, NEAR], [0, T]], base=NEAR, channel_multiplier=0,
                           allow_small_or_imprecise_dtypes=True).then_inc(sort_consts, 1)
            nc.gpsimd.iota(rec[:, :, 0], [[P, T]], base=0, channel_multiplier=1).then_inc(rec_rows, 1)
            pool.wait_ge(before_zero, 1)
            nc.gpsimd.affine_select(out=before[:], in_=before[:], compare_op=ALU.is_gt, fill=-1.0, base=0,
                                    pattern=[[1, P]], channel_multiplier=-1).then_inc(sort_consts, 1)

            pool.wait_ge(rank_ok, 1)
            pool.wait_ge(decoded, (T // 4) * STEPS)
            pool.wait_ge(rec_rows, 1)
            for t in range(T):
                nc.gpsimd.indirect_dma_start(order[:, :], bass.IndirectOffsetOnAxis(ap=rank[:, t:t + 1], axis=0),
                                             rec[:, t, :], None).then_inc(order_out, 16)

            for s in range(4):
                pool.wait_ge(rows_out[s], 32 * (T // 4))
            pool.wait_ge(near_ok, 1)

            def fetch(Q, u, c, first=False):
                t = Q * 4 + u
                s = side_of(u)
                n = 0 if first and u == 0 else s
                if first and u in (3,):
                    pool.wait_ge(pv_ps, 1)
                if not first:
                    pool.wait_ge(pv_ps, t - 3)
                if not first:
                    pool.wait_ge(joined, t - 3)
                    pool.sem_inc(passed_pool, 1)
                nc.gpsimd.tensor_copy(near_q[:, s, :], near[:, t, :]).then_inc(near_copied, 1)
                pool.wait_ge(near_copied, t + 1)
                pool.sem_inc(passed_pool, 1)
                nc.gpsimd.indirect_dma_start(row[:, s, 2 * HK:], None, qx[:, :],
                                             bass.IndirectOffsetOnAxis(ap=near_q[:, s, 0:1], axis=0)).then_inc(qx_in[s], 16)
                g = gathered(u, c, first and u == 0)
                for a in range(c):
                    nc.gpsimd.indirect_dma_start(g[:, a, :], None, kv[:, :],
                                                 bass.IndirectOffsetOnAxis(ap=near_q[:, s, 1 + a:2 + a], axis=0)).then_inc(kv_in[s], 16)

            def give(Q, u):
                t = Q * 4 + u
                s = side_of(u)
                pool.wait_ge(normed, t + 1)
                pool.sem_inc(passed_pool, 1)
                nc.gpsimd.tensor_copy(out_q[:, s, :], near[:, t, 0:1]).then_inc(outq_copied, 1)
                pool.wait_ge(outq_copied, t + 1)
                pool.sem_inc(passed_pool, 1)
                nc.gpsimd.indirect_dma_start(out[:, :], bass.IndirectOffsetOnAxis(ap=out_q[:, s, 0:1], axis=0),
                                             joined_sb[:, s, :], None).then_inc(given[s], 16)

            for q0, nq, cs, _ in TURNS:
                if q0 == 0:
                    for u in range(4):
                        fetch(0, u, cs[u], first=True)
                elif q0 == 1:
                    for u in range(4):
                        fetch(1, u, cs[u])
                        if u:
                            give(0, u - 1)
                else:
                    with pool.Fori(q0, q0 + nq) as Q:
                        for u in range(4):
                            fetch(Q, u, cs[u])
                            give(Q - 2 if u == 0 else Q - 1, (u + 3) % 4)
            for u in range(3, 8):
                give(T // 4 - 2 + u // 4, u % 4)
            for s in range(SIDES):
                pool.wait_ge(given[s], 16 * (T // 4))
            pool.sem_inc(sparse_done, 1)

        @block.tensor
        def _(pe):
            pe.wait_ge(ident_ok, 1)
            pe.wait_ge(digits_ok, 2 + DIGITS)
            pe.wait_ge(column_in, 16)
            pe.wait_ge(w_in, 16 * 3 * DC)

            def step(i, s, first=False):
                t = i * 4 + s
                pe.wait_ge(diag_ok, t + 1)
                if not first or s >= 2:
                    pe.wait_ge(keys_ok, t - 1)
                packed_ps = banks[PACK + s % 2][:]
                halves = adj_sb[:, s, :].bitcast(bf16).rearrange("p (m two) -> p m two", two=2)
                for k in range(DIGITS):
                    nc.tensor.matmul(packed_ps, digit[:, k, :], halves[:, k * BANK:(k + 1) * BANK, 1],
                                     start=(k == 0), stop=False)
                nc.tensor.matmul(packed_ps, ones2[:], column[:], start=False, stop=True).then_inc(packed, 1)
                pe.wait_ge(x_in[s], i * 16 + 16)
                for c in range(DC):
                    last = nc.tensor.transpose(banks[XT + s % 2][:, c * P:(c + 1) * P],
                                               row[:, s, 3 * HK + c * P:3 * HK + (c + 1) * P], ident[:])
                last.then_inc(xT_ps, 1)
                pe.wait_ge(xT_ok, t + 1)
                for j in range(3):
                    if not (first and s == 0):
                        if j < 2:
                            pe.wait_ge(kv_copied, t * 2 - 1 + j)
                        else:
                            pe.wait_ge(q_copied, t)
                    for c in range(DC):
                        last = nc.tensor.matmul(banks[KVQ + j][:], xT[:, s % 2, c, :], w[:, c, j * HK:(j + 1) * HK],
                                                start=(c == 0), stop=(c == DC - 1))
                    last.then_inc(kvq_ps, 1)

            for s in range(4):
                step(0, s, first=True)
            with pe.Fori(1, T // 4) as i:
                for s in range(4):
                    step(i, s)

            pe.wait_ge(sort_consts, 3)
            pe.wait_ge(onehot_ok, 1)
            nc.tensor.matmul(banks[0][:], ones[:], onehot[:].rearrange("p d t -> p (d t)"), start=True, stop=True)
            nc.tensor.matmul(banks[1][:], before[:], onehot[:].rearrange("p d t -> p (d t)"), start=True,
                             stop=True).then_inc(place_ps, 1)

            pe.wait_ge(bad_ok, 1)
            nc.tensor.matmul(banks[5][:, 0:NBAD], ones_f[:, 0:P], bad[:], start=True, stop=True).then_inc(bad_ps, 1)

            pe.wait_ge(wo_in, 16)

            def attend(Q, u, c, first=False):
                t = Q * 4 + u
                pe.wait_ge(weighted, t + 1)
                g = gathered(u, c, first and u == 0)
                for a in range(c):
                    last = nc.tensor.matmul(banks[O_PS][:], ident[:], g[:, a, HK:], start=(a == 0), stop=(a == c - 1))
                last.then_inc(pv_ps, 1)
                pe.wait_ge(o_copied, t + 1)
                for k in range(HC):
                    last = nc.tensor.transpose(banks[OT_PS][:, k * P:(k + 1) * P], o_sb[:, k * P:(k + 1) * P], ident[:])
                last.then_inc(oT_ps, 1)
                if not (first and u < 2):
                    pe.wait_ge(joined, t - 1)
                pe.wait_ge(oT_copied, t + 1)
                for k in range(HC):
                    last = nc.tensor.matmul(banks[Y_PS + u % 2][:, 0:D], oT_sb[:, k, :], wo_sb[:, k, :],
                                            start=(k == 0), stop=(k == HC - 1))
                last.then_inc(y_ps, 1)

            for q0, nq, cs, _ in TURNS:
                if nq == 1:
                    for u in range(4):
                        attend(q0, u, cs[u], first=(q0 == 0))
                else:
                    with pe.Fori(q0, q0 + nq) as Q:
                        for u in range(4):
                            attend(Q, u, cs[u])

            pe.wait_ge(flag_ok, 1)
            crowded = pe.value_load(flag[0:1, 0:1], min_val=0, max_val=1 << 20)
            pe.wait_ge(sparse_done, 1)
            with pe.If(crowded > 0):
                for count in (g_head_done, g_kT_ps, g_qT_ps, g_pT_ps, g_pv, g_s_ps):
                    pe.sem_inc(count, 1)
                with pe.Fori(0, H) as h:
                    with pe.Fori(0, NB) as b:
                        pe.wait_ge(g_k_in, (h * NB + b + 1) * 16)
                        pe.wait_ge(g_kT_ok, h * NB + b + 1)
                        pe.sem_inc(passed_pe, 1)
                        for j in range(4):
                            last = nc.tensor.transpose(banks[0][0:KD, j * P:(j + 1) * P], k_nat[:, j, :], ident[:])
                        last.then_inc(g_kT_ps, 1)
                    pe.wait_ge(g_kT_ok, (h + 1) * NB + 1)
                    pe.wait_ge(g_head_in, (h + 1) * 32)
                    pe.sem_inc(passed_pe, 1)
                    with pe.Fori(0, T) as t:
                        n = h * T + t
                        pe.wait_ge(g_q_in, (n + 1) * 16)
                        pe.sem_inc(passed_pe, 1)
                        nc.tensor.transpose(banks[1][0:KD, 0:P], q_nat[:], ident[:]).then_inc(g_qT_ps, 1)
                        pe.wait_ge(g_qT_ok, n + 1)
                        for c in range(NB):
                            if c < 2:
                                pe.wait_ge(g_logits, n * NB + 1)
                            else:
                                pe.wait_ge(g_logits, n * NB + c - 1 + 1)
                            nc.tensor.matmul(banks[2 + c % 2][:], qT[:], kT[:, c * BANK:(c + 1) * BANK],
                                             start=True, stop=True).then_inc(g_s_ps, 1)
                        pe.wait_ge(g_exp, n + 1)
                        pe.wait_ge(g_o, n + 1)
                        for c in range(NB):
                            if c < 2:
                                pe.wait_ge(g_pT_ok, n * NB + 1)
                            else:
                                pe.wait_ge(g_pT_ok, n * NB + c - 1 + 1)
                            for j in range(4):
                                last = nc.tensor.transpose(banks[4 + c % 2][:, j * P:(j + 1) * P],
                                                           logits[:, (4 * c + j) * P:(4 * c + j + 1) * P], ident[:])
                            last.then_inc(g_pT_ps, 1)
                            pe.wait_ge(g_pT_ok, n * NB + c + 1 + 1)
                            for j in range(4):
                                last = nc.tensor.matmul(banks[6][:, 0:KD], pT[:, c % 2, j * P:(j + 1) * P], vh[:, 4 * c + j, :],
                                                        start=(c + j == 0), stop=(c == NB - 1 and j == 3))
                            last.then_inc(g_pv, 1)
                        pe.wait_ge(g_o, n + 1 + 1)
                        pe.sem_inc(passed_pe, 1)
                        nc.tensor.transpose(banks[1][0:KD, 0:P], o_n[:], ident[:]).then_inc(g_oT_ps, 1)
                        pe.wait_ge(g_oT_ok, n + 1)
                        pe.wait_ge(g_res, n + 1)
                        nc.tensor.matmul(banks[7][:, 0:D], oT[:], woh[:], start=True, stop=True).then_inc(g_head_done, 1)

        @block.scalar
        def _(act):
            nc.scalar.preload_act_table_set("natural_log_exp_and_others")

            def step(i, s, first=False):
                t = i * 4 + s
                act.wait_ge(xT_ps, t + 1)
                if not first or s >= 2:
                    act.wait_ge(kvq_ps, t * 3 - 3)
                nc.scalar.copy(xT[:, s % 2, :, :], banks[XT + s % 2][:, 0:D].rearrange("p (c q) -> p c q", c=DC)).then_inc(xT_ok, 1)
                if not first:
                    act.wait_ge(rows_out[s], i * 32)
                for j in range(2):
                    act.wait_ge(kvq_ps, t * 3 + j + 1)
                    nc.scalar.copy(row[:, s, j * HK:(j + 1) * HK], banks[KVQ + j][:]).then_inc(kv_copied, 1)

            for s in range(4):
                step(0, s, first=True)
            with act.Fori(1, T // 4) as i:
                for s in range(4):
                    step(i, s)

            act.wait_ge(eps_ok, 1)

            def weights(Q, u, c):
                t = Q * 4 + u
                s = side_of(u)
                act.wait_ge(shifted, t + 1)
                nc.scalar.activation(pr[:, s, 0:c, :], lg[:, s, 0:c, :], ACT.Exp).then_inc(exps, 1)

            def copies(Q, u):
                t = Q * 4 + u
                act.wait_ge(pv_ps, t + 1)
                nc.scalar.copy(o_sb[:], banks[O_PS][:]).then_inc(o_copied, 1)
                act.wait_ge(oT_ps, t + 1)
                nc.scalar.copy(oT_sb[:].rearrange("p c q -> p (c q)"), banks[OT_PS][:]).then_inc(oT_copied, 1)

            def deviation(Q, u):
                t = Q * 4 + u
                s = side_of(u)
                act.wait_ge(moments, t + 1)
                nc.scalar.activation(lnv[:, s, :], mv4[:, s, 1:2], ACT.Ln, bias=eps[:, 0:1]).then_inc(ln_ok, 1)
                act.wait_ge(ln_ok, t + 1)
                nc.scalar.activation(rs4[:, s, :], lnv[:, s, :], ACT.Exp, scale=-0.5).then_inc(rs_ok, 1)

            def act_quad(Q, cs, first=False):
                for u in range(4):
                    weights(Q, u, cs[u])
                    if not (first and u == 0):
                        copies(Q if u else Q - 1, (u + 3) % 4)
                    if not (first and u < 2):
                        deviation(Q if u >= 2 else Q - 1, (u + 2) % 4)

            for q0, nq, cs, _ in TURNS:
                if nq == 1:
                    act_quad(q0, cs, first=(q0 == 0))
                else:
                    with act.Fori(q0, q0 + nq) as Q:
                        act_quad(Q, cs)
            copies(T // 4 - 1, 3)
            deviation(T // 4 - 1, 2)
            deviation(T // 4 - 1, 3)

            act.wait_ge(flag_ok, 1)
            crowded = act.value_load(flag[0:1, 0:1], min_val=0, max_val=1 << 20)
            act.wait_ge(sparse_done, 1)
            with act.If(crowded > 0):
                for count in (g_kT_ok, g_pT_ok):
                    act.sem_inc(count, 1)
                with act.Fori(0, H) as h:
                    with act.Fori(0, NB) as b:
                        act.wait_ge(g_kT_ps, h * NB + b + 1 + 1)
                        act.wait_ge(g_head_done, h * T + 1)
                        nc.scalar.copy(kT[:, bass.ds(b * BANK, BANK)], banks[0][0:KD, :]).then_inc(g_kT_ok, 1)
                    with act.Fori(0, T) as t:
                        n = h * T + t
                        act.wait_ge(g_qT_ps, n + 1 + 1)
                        act.wait_ge(g_s_ps, n * NB + 1)
                        nc.scalar.copy(qT[:], banks[1][0:KD, 0:P]).then_inc(g_qT_ok, 1)
                        act.wait_ge(g_max, n + 1)
                        nc.scalar.activation(logits[:], logits[:], ACT.Exp, bias=nmax[:, 0:1],
                                             accum_out=rsum[:, 0:1]).then_inc(g_exp, 1)
                        for c in range(NB):
                            act.wait_ge(g_pT_ps, n * NB + c + 1 + 1)
                            if c < 2:
                                act.wait_ge(g_pv, n * NB + 1)
                            else:
                                act.wait_ge(g_pv, n * NB + c - 1 + 1)
                            nc.scalar.copy(pT[:, c % 2, :], banks[4 + c % 2][:]).then_inc(g_pT_ok, 1)
                        act.wait_ge(g_oT_ps, n + 1)
                        nc.scalar.copy(oT[:], banks[1][0:KD, 0:P]).then_inc(g_oT_ok, 1)
                act.wait_ge(eps_ok, 1)
                with act.Fori(0, T) as t:
                    act.wait_ge(g_mv, t + 1)
                    nc.scalar.activation(std[:], mv[:, 1:2], ACT.Sqrt, bias=eps[:, 0:1]).then_inc(g_std, 1)

        @block.vector
        def _(dve):
            chain = [0]

            def after(ins):
                chain[0] += 1
                ins.then_inc(dve_chain, 1)
                dve.wait_ge(dve_chain, chain[0])

            nc.vector.memset(ones2[:], 1.0).then_inc(digits_ok, 1)
            nc.vector.memset(ones_f[:], 1.0).then_inc(digits_ok, 1)
            nc.vector.memset(eps[:], EPS).then_inc(eps_ok, 1)
            dve.wait_ge(ident_ok, 1)
            for k in range(DIGITS):
                nc.vector.tensor_scalar(digit[:, k, :], ident[:], float(KEY << k), None, ALU.mult).then_inc(digits_ok, 1)

            def itself(i, s):
                dve.wait_ge(adj_in[s], i * 16 + 16)
                d = adj_sb[:, s, bass.ds((i * 4 + s) * P, P)]
                nc.vector.tensor_tensor(d, d, ident[:], ALU.max).then_inc(diag_ok, 1)

            def step(i, s, first=False, last=False):
                t = i * 4 + s
                if not (last and s == 3):
                    itself(i + (s == 3), (s + 1) % 4)
                dve.wait_ge(packed, t + 1)
                dve.sem_inc(passed_dve, 1)
                for g in range(SEGS):
                    last = nc.vector.max(keys[:, s, g * 8:(g + 1) * 8], banks[PACK + s % 2][:, g * SEG:(g + 1) * SEG])
                last.then_inc(keys_ok, 1)
                if not first:
                    dve.wait_ge(rows_out[s], i * 32)
                dve.wait_ge(kvq_ps, t * 3 + 3)
                nc.vector.tensor_copy(row[:, s, 2 * HK:3 * HK], banks[KVQ + 2][:]).then_inc(q_copied, 1)

            def decode(i):
                n = [0]

                def count(ins):
                    n[0] += 1
                    ins.then_inc(decoded, 1)

                def settle():
                    dve.wait_ge(decoded, i * STEPS + n[0])

                four = bass.ds(i * 4, 4)
                dve.wait_ge(keys_ok, i * 4 + 4)
                count(nc.vector.tensor_scalar(col[:], keys[:], KEY - 1, None, ALU.bitwise_and))
                count(nc.vector.tensor_scalar(bits[:], keys[:], KEY.bit_length() - 1, None, ALU.logical_shift_right))
                settle()
                count(nc.vector.tensor_copy(val[:, 0, :, :], bits[:]))
                eighth = bits[:].rearrange("p t (g e) -> p t g e", e=8)[:, :, :, 7]
                count(nc.vector.tensor_reduce(crowd[:, bass.ds(i, 1)], eighth, AX.XY, ALU.max))
                settle()
                for lv in range(LEVELS):
                    raw = val[:, lv, :, :].bitcast(i32)
                    count(nc.vector.tensor_scalar(power[:], raw, 0x7F800000, None, ALU.bitwise_and))
                    count(nc.vector.tensor_scalar(expo[:], raw, 23, None, ALU.logical_shift_right))
                    settle()
                    count(nc.vector.scalar_tensor_tensor(out=cand[:, :, lv * SEGS * 8:(lv + 1) * SEGS * 8], in0=expo[:],
                                                         scalar=float(KEY), in1=col[:], op0=ALU.mult, op1=ALU.add))
                    count(nc.vector.tensor_tensor(val[:, lv + 1, :, :], val[:, lv, :, :], power[:].bitcast(fp32),
                                                  ALU.subtract))
                    settle()
                count(nc.vector.tensor_reduce(crowd[:, bass.ds(i + T // 4, 1)], val[:, LEVELS, :, :], AX.XY, ALU.max))
                dve.sem_inc(passed_dve, 1)
                for j in range(4):
                    count(nc.vector.max(top[:, j, 0:8], cand[:, j, :]))
                settle()
                dve.sem_inc(passed_dve, 1)
                for j in range(4):
                    count(nc.vector.match_replace(cand2[:, j, :], top[:, j, 0:8], cand[:, j, :], 0.0))
                settle()
                dve.sem_inc(passed_dve, 1)
                for j in range(4):
                    count(nc.vector.max(top[:, j, 8:16], cand2[:, j, :]))
                settle()
                count(nc.vector.tensor_scalar(rec[:, four, 1:], top[:], float(-BIAS), None, ALU.add))
                count(nc.vector.tensor_scalar(listed[:], top[:], float(BIAS), None, ALU.is_ge))
                settle()
                count(nc.vector.tensor_reduce(degree[:, four], listed[:], AX.X, ALU.add))
                assert n[0] == STEPS

            itself(0, 0)
            for s in range(4):
                step(0, s, first=True)
            decode(0)
            with dve.Fori(1, T // 4 - 1) as i:
                for s in range(4):
                    step(i, s)
                decode(i)
            for s in range(4):
                step(T // 4 - 1, s, last=True)
            decode(T // 4 - 1)

            dve.wait_ge(decoded, (T // 4) * STEPS)
            dve.wait_ge(sort_consts, 3)
            nc.vector.tensor_tensor(onehot[:], degree[:].unsqueeze(1).to_broadcast([P, NEAR, T]), degrees[:],
                                    ALU.is_equal).then_inc(onehot_ok, 1)
            dve.wait_ge(place_ps, 1)
            flat = place[:].rearrange("p d t -> p (d t)")
            after(nc.vector.tensor_tensor_scan(flat, ones_f[:], banks[0][:], 0.0, ALU.mult, ALU.add))
            after(nc.vector.tensor_tensor(flat, flat, banks[1][:], ALU.add))
            after(nc.vector.tensor_tensor(flat, flat, onehot[:].rearrange("p d t -> p (d t)"), ALU.mult))
            with nc.allow_low_precision(reason="whole numbers below N"):
                nc.vector.tensor_reduce(rank[:], place[:].rearrange("p d t -> p t d"), AX.X, ALU.add).then_inc(rank_ok, 1)

            dve.wait_ge(order_in, 16)
            nc.vector.tensor_scalar(near[:], srt[:], 0.0, None, ALU.max).then_inc(near_ok, 1)
            after(nc.vector.tensor_scalar(mask[:], srt[:, :, 1:], 0.0, -BIG, ALU.is_lt, ALU.mult))

            nc.vector.tensor_scalar(bad[:, 0:T // 4], crowd[:, 0:T // 4], 1.0, None, ALU.is_ge)
            nc.vector.tensor_scalar(bad[:, T // 4:T // 2], crowd[:, T // 4:], 0.0, None, ALU.is_gt)
            for n, (t0, t1, c) in enumerate(LIMITS):
                last = nc.vector.tensor_reduce(excess[:, n:n + 1], srt[:, t0:t1, 1 + c], AX.X, ALU.max)
            after(last)
            nc.vector.tensor_scalar(bad[:, T // 2:], excess[:], 0.0, None, ALU.is_ge).then_inc(bad_ok, 1)
            dve.wait_ge(bad_ps, 1)
            with nc.allow_low_precision(reason="a count"):
                nc.vector.tensor_reduce(flag[:], banks[5][:, 0:NBAD], AX.X, ALU.add).then_inc(flag_ok, 1)

            def score(Q, u, c, arrivals, q0):
                t = Q * 4 + u
                s = side_of(u)
                g = gathered(u, c, c == FIRST)[:, :, 0:HK]
                dve.wait_ge(qx_in[s], Q * 16 + 16)
                dve.wait_ge(kv_in[s], (Q - q0) * (16 * c) + (arrivals[s] + c) * 16)
                nc.vector.tensor_tensor(g, g, row[:, s, 2 * HK:3 * HK].unsqueeze(1).to_broadcast([P, c, HK]),
                                        ALU.mult).then_inc(products, 1)
                dve.wait_ge(products, t + 1)
                l = lg[:, s, 0:c, :]
                nc.vector.tensor_reduce(l, g.rearrange("p c (h k) -> p c h k", h=H), AX.X, ALU.add).then_inc(scores, 1)
                dve.wait_ge(scores, t + 1)
                nc.vector.scalar_tensor_tensor(out=l, in0=l, scalar=SCALE,
                                               in1=mask[:, t, 0:c].unsqueeze(2).to_broadcast([P, c, H]),
                                               op0=ALU.mult, op1=ALU.add).then_inc(masked, 1)
                dve.wait_ge(masked, t + 1)
                nc.vector.tensor_reduce(mx[:, s, :], l.rearrange("p c h -> p h c"), AX.X, ALU.max).then_inc(maxima, 1)
                dve.wait_ge(maxima, t + 1)
                nc.vector.tensor_tensor(l, l, mx[:, s, :].unsqueeze(1).to_broadcast([P, c, H]),
                                        ALU.subtract).then_inc(shifted, 1)

            def weigh(Q, u, c):
                t = Q * 4 + u
                s = side_of(u)
                g = gathered(u, c, c == FIRST)[:, :, HK:].rearrange("p c (h k) -> p c h k", h=H)
                p = pr[:, s, 0:c, :]
                dve.wait_ge(exps, t + 1)
                nc.vector.tensor_reduce(sm[:, s, :], p.rearrange("p c h -> p h c"), AX.X, ALU.add).then_inc(sums, 1)
                dve.wait_ge(sums, t + 1)
                nc.vector.reciprocal(inv[:, s, :], sm[:, s, :]).then_inc(inverses, 1)
                dve.wait_ge(inverses, t + 1)
                nc.vector.tensor_tensor(p, p, inv[:, s, :].unsqueeze(1).to_broadcast([P, c, H]), ALU.mult).then_inc(probs, 1)
                dve.wait_ge(probs, t + 1)
                nc.vector.tensor_tensor(g, g, p.unsqueeze(3).to_broadcast([P, c, H, KD]), ALU.mult).then_inc(weighted, 1)

            def join(Q, u, first=False):
                t = Q * 4 + u
                s = side_of(u)
                dve.wait_ge(y_ps, t + 1)
                if not first:
                    dve.wait_ge(given[s], Q * 16)
                nc.vector.tensor_tensor(joined_sb[:, s, :], banks[Y_PS + u % 2][:, 0:D], row[:, s, 3 * HK:], ALU.add).then_inc(joined, 1)
                dve.wait_ge(joined, t + 1)
                nc.vector.bn_stats(st[:, s, :], joined_sb[:, s, :]).then_inc(half_moments, 1)
                dve.wait_ge(half_moments, t + 1)
                dve.sem_inc(passed_dve, 1)
                nc.vector.bn_aggr(mv4[:, s, :], st[:, s, :]).then_inc(moments, 1)

            def norm(Q, u):
                t = Q * 4 + u
                s = side_of(u)
                dve.wait_ge(rs_ok, t + 1)
                dve.wait_ge(moments, t + 1)
                nc.vector.tensor_scalar(joined_sb[:, s, :], joined_sb[:, s, :], mv4[:, s, 0:1], rs4[:, s, 0:1],
                                        ALU.subtract, ALU.mult).then_inc(normed, 1)

            def quad(Q, cs, arrivals, q0, first=False):
                for u in range(4):
                    score(Q, u, cs[u], arrivals, q0)
                    if u:
                        weigh(Q, u - 1, cs[u - 1])
                    if not (first and u < 2):
                        join(Q if u >= 2 else Q - 1, (u + 2) % 4, first or q0 == 1 and u < 2)
                    if not (first and u < 3):
                        norm(Q if u == 3 else Q - 1, (u + 1) % 4)
                weigh(Q, 3, cs[3])

            for q0, nq, cs, arrivals in TURNS:
                if nq == 1:
                    quad(q0, cs, arrivals, q0, first=(q0 == 0))
                else:
                    with dve.Fori(q0, q0 + nq) as Q:
                        quad(Q, cs, arrivals, q0)
            Q = T // 4 - 1
            join(Q, 2)
            norm(Q, 1)
            join(Q, 3)
            norm(Q, 2)
            norm(Q, 3)

            dve.wait_ge(flag_ok, 1)
            crowded = dve.value_load(flag[0:1, 0:1], min_val=0, max_val=1 << 20)
            dve.wait_ge(sparse_done, 1)
            with dve.If(crowded > 0):
                for count in (g_logits, g_o, g_res):
                    dve.sem_inc(count, 1)
                dve.wait_ge(g_res_in, 16)
                with dve.Fori(0, H) as h:
                    with dve.Fori(0, T) as t:
                        n = h * T + t
                        dve.wait_ge(g_adj_in, (n + 1) * 16)
                        nc.vector.tensor_tensor(logits[:, bass.ds(t * P, P)], logits[:, bass.ds(t * P, P)], ident[:],
                                                ALU.max).then_inc(g_diag, 1)
                        dve.wait_ge(g_diag, n + 1)
                        nc.vector.tensor_scalar(logits[:], logits[:], -1.0, BIG, ALU.add, ALU.mult).then_inc(g_bias, 1)
                        dve.wait_ge(g_bias, n + 1)
                        for c in range(NB):
                            dve.wait_ge(g_s_ps, n * NB + c + 1 + 1)
                            piece = logits[:, c * BANK:(c + 1) * BANK]
                            nc.vector.scalar_tensor_tensor(out=piece, in0=banks[2 + c % 2][:], scalar=SCALE, in1=piece,
                                                           op0=ALU.mult, op1=ALU.add).then_inc(g_logits, 1)
                        dve.wait_ge(g_logits, (n + 1) * NB + 1)
                        nc.vector.tensor_reduce(nmax[:], logits[:], AX.X, ALU.max, negate=True).then_inc(g_max, 1)
                        dve.wait_ge(g_exp, n + 1)
                        nc.vector.reciprocal(rinv[:], rsum[:]).then_inc(g_rinv, 1)
                        dve.wait_ge(g_rinv, n + 1)
                        dve.wait_ge(g_pv, (n + 1) * NB + 1)
                        nc.vector.tensor_scalar(o_n[:], banks[6][:, 0:KD], rinv[:, 0:1], None, ALU.mult).then_inc(g_o, 1)
                        dve.wait_ge(g_head_done, n + 1 + 1)
                        r = res[:, bass.ds(t, 1), :].rearrange("p a d -> p (a d)")
                        nc.vector.tensor_tensor(r, r, banks[7][:, 0:D], ALU.add).then_inc(g_res, 1)
                dve.wait_ge(g_res, H * T + 1)
                with dve.Fori(0, T) as t:
                    r = res[:, bass.ds(t, 1), :].rearrange("p a d -> p (a d)")
                    nc.vector.bn_stats(stats[:], r).then_inc(g_stats, 1)
                    dve.wait_ge(g_stats, t + 1)
                    dve.sem_inc(passed_dve, 1)
                    nc.vector.bn_aggr(mv[:], stats[:]).then_inc(g_mv, 1)
                    dve.wait_ge(g_std, t + 1)
                    nc.vector.reciprocal(rstd[:], std[:]).then_inc(g_rstd, 1)
                    dve.wait_ge(g_rstd, t + 1)
                    dve.wait_ge(g_mv, t + 1)
                    nc.vector.tensor_scalar(r, r, mv[:, 0:1], rstd[:, 0:1], ALU.subtract, ALU.mult).then_inc(g_ln, 1)


_INS = ['x', 'adj', 'L0_gnn_Wks', 'L0_gnn_Wqs', 'L0_gnn_Wvs', 'L0_gnn_Wo']


def kernel(**inputs):
    import numpy as _np
    import concourse.bacc as _bacc
    from concourse import mybir as _mybir
    from concourse.bass_utils import run_bass_kernel_spmd as _run

    nc = _bacc.Bacc("TRN2", target_bir_lowering=False, num_devices=1)
    arrays, args = {}, []
    for name in _INS:
        a = _np.ascontiguousarray(inputs[name])
        arrays[f"in_{name}_dram"] = a
        args.append(nc.dram_tensor(f"in_{name}_dram", a.shape, _mybir.dt.from_np(a.dtype), kind="ExternalInput").ap())
    shape = inputs['x'].shape
    args.append(nc.dram_tensor("out_0_dram", shape, _mybir.dt.float32, kind="ExternalOutput").ap())
    graph_attention_resnorm_kernel(nc, *args)
    r = _run(nc, [arrays], core_ids=[0])
    return r.results[0]["out_0_dram"]
```

```python
import numpy as np
import concourse.bass as bass
from concourse import mybir
from contextlib import ExitStack


def graph_attention_resnorm_kernel(nc, x, adj, wks, wqs, wvs, wo, out):
    fp32 = mybir.dt.float32
    bf16 = mybir.dt.bfloat16
    i32 = mybir.dt.int32
    u32 = mybir.dt.uint32
    ALU = mybir.AluOpType
    ACT = mybir.ActivationFunctionType
    AX = mybir.AxisListType

    P = 128
    N, D = x.shape
    H, _, KD = wks.shape
    HK = H * KD
    T = N // P
    DC = D // P
    HC = HK // P
    EPS = 1e-5
    BIG = 1e16
    SCALE = float(KD) ** -0.5
    BANK = 512
    NB = N // BANK

    DIGITS = N // BANK
    KEY = BANK
    SEGS = 4
    SEG = BANK // SEGS
    LEVELS = 3
    BIAS = 127 * KEY
    NEAR = 16
    CAND = LEVELS * SEGS * 8
    GT = 16
    G = T // GT
    CAPS = [12, 5, 5, 4, 4, 4, 3, 3, 3, 3, 2, 2, 2, 2, 2, 1]
    LIMITS = [(0, 1, 12), (1, 3, 5), (3, 6, 4), (6, 10, 3), (10, 15, 2), (15, 16, 1)]
    ORDER = [15, 12, 7, 13, 3, 10, 2, 9, 11, 0, 14, 5, 4, 8, 1, 6]
    ORDER += [GT + i for i in (2, 11, 12, 8, 4, 3, 10, 13, 1, 7, 5, 6, 14, 9, 15, 0)]
    CAP = [CAPS[i % GT] for i in ORDER]
    SLOTS = 25

    def rooms():
        user = [-1] * SLOTS
        plan = []
        for t, c in enumerate(CAP):
            a = min(range(SLOTS - c + 1), key=lambda a: (max(user[a:a + c]), a))
            plan.append((a, max(user[a:a + c]) + 1))
            user[a:a + c] = [t] * c
        return plan

    ROOM = rooms()
    PIECE = 6
    WEIGHED = 3
    TURNS, TILES, SCANS, BATCH = 4, 8, 6, 3
    EARLY = TURNS * SCANS + 1
    BATCHES = [(a, min(BATCH, T - a)) for a in range(0, T, BATCH)]
    STEPS = 4 + 4 * LEVELS + 1 + 3 * BATCH + 3
    NBAD = 2 * len(BATCHES) + G * len(LIMITS)
    RING = 8
    SIDES = 4
    RESULTS = 5
    X_AHEAD = 2
    LAG = 7
    LATE_FROM = 0
    SORT_AT = 8
    ORDER_AT = 10
    ORDER_PARTS = 1
    LISTS_AT = 11
    HALF = N // 2

    kv = nc.dram_tensor("kv_table", (N, 2 * HK), fp32, kind="Internal").ap()
    order = nc.dram_tensor("order_table", (N, 1 + NEAR), i32, kind="Internal").ap()

    ctx = ExitStack()
    with ctx:
        def sb(name, shape, dt=fp32):
            return ctx.enter_context(nc.sbuf_tensor(name, shape, dt))

        def sem(name):
            return ctx.enter_context(nc.semaphore(name))

        ident = sb("ident", [P, P])
        digit = sb("digit", [P, DIGITS, P], bf16)
        column = sb("column", [2, BANK], bf16)
        column_lo = sb("column_lo", [1, BANK], bf16)
        ones2 = sb("ones2", [2, P], bf16)
        ones = sb("ones", [P, P], bf16)
        before = sb("before", [P, P], bf16)
        ones_f = sb("ones_f", [P, NEAR * GT])
        degrees = sb("degrees", [P, NEAR, GT])
        nodes = sb("nodes", [P, T], i32)
        w = sb("w", [P, DC, 3 * HK])
        wo_sb = sb("wo_sb", [P, HC, D])
        eps = sb("eps", [P, 1])
        adj_sb = sb("adj_sb", [P, 2, 2, HALF])
        row = sb("row", [P, SIDES, 2 * HK + D])
        xT = sb("xT", [P, 2, DC, P])
        arena = sb("arena", [P, SLOTS, 2 * HK])
        keys = sb("keys", [P, BATCH, SEGS * 8], i32)
        col = sb("col", [P, BATCH, SEGS * 8], i32)
        bits = sb("bits", [P, BATCH, SEGS * 8], i32)
        val = sb("val", [P, LEVELS + 1, BATCH, SEGS * 8])
        expo = sb("expo", [P, BATCH, SEGS * 8], i32)
        power = sb("power", [P, BATCH, SEGS * 8], i32)
        cand = sb("cand", [P, BATCH, CAND])
        cand2 = sb("cand2", [P, BATCH, CAND])
        top = sb("top", [P, BATCH, NEAR])
        listed = sb("listed", [P, BATCH, NEAR])
        rec = sb("rec", [P, T, 1 + NEAR], i32)
        degree = sb("degree", [P, T])
        onehot = sb("onehot", [P, NEAR, GT], bf16)
        place = sb("place", [P, NEAR, GT])
        base = sb("base", [P, 1])
        rank = sb("rank", [P, T], i32)
        srt = sb("srt", [P, T, 1 + NEAR], i32)
        near = sb("near", [P, T, 1 + NEAR], i32)
        mask = sb("mask", [P, T, NEAR])
        crowd = sb("crowd", [P, 2 * len(BATCHES)])
        excess = sb("excess", [P, G * len(LIMITS)])
        bad = sb("bad", [P, NBAD])
        flag = sb("flag", [P, 1], i32)
        spent = row[:].rearrange("p b c -> p (b c)")
        prod = spent[:, 0:PIECE * HK].rearrange("p (a c) -> p a c", c=HK)
        xq = spent[:, PIECE * HK:PIECE * HK + RING * D].rearrange("p (u d) -> p u d", d=D)
        lg = sb("lg", [P, SIDES, CAPS[0], H])
        pr = sb("pr", [P, SIDES, CAPS[0], H])
        mx = sb("mx", [P, SIDES, H])
        sm = sb("sm", [P, SIDES, H])
        inv = sb("inv", [P, SIDES, H])
        o_sb = sb("o_sb", [P, HK])
        oT_sb = sb("oT_sb", [P, HC, P])
        joined_sb = sb("joined_sb", [P, RESULTS, D])
        lnv = sb("lnv", [P, SIDES, 1])
        rs4 = sb("rs4", [P, SIDES, 1])
        less = sb("less", [P, SIDES, 1])
        total = sb("total", [P, SIDES, 1])
        squares = sb("squares", [P, SIDES, 1])
        square = sb("square", [P, D])
        shift = sb("shift", [P, SIDES, 1])
        logits = adj_sb[:, 0, :, :].rearrange("p h m -> p (h m)")
        kT = adj_sb[0:KD, 1, :, :].rearrange("p h m -> p (h m)")
        spare = arena[:].rearrange("p a c -> p (a c)")
        taken = [0]

        def carve(shape):
            n = int(np.prod(shape[1:]))
            v = spare[0:shape[0], taken[0]:taken[0] + n]
            taken[0] += n
            return v.rearrange("p (a c) -> p a c", c=shape[2]) if len(shape) == 3 else v

        vh = carve([P, T, KD])
        res = carve([P, T, D])
        woh = carve([KD, D])
        k_nat = carve([P, 4, KD])
        wqh = carve([P, DC, KD])
        x_nat = carve([P, D])
        x_natT = carve([P, DC, P])
        qT = carve([KD, P])
        pT = carve([P, 2, BANK])
        o_n = carve([P, KD])
        oT = carve([KD, P])
        nmax = sb("nmax", [P, 1])
        rsum = sb("rsum", [P, 1])
        rinv = sb("rinv", [P, 1])
        stats = sb("stats", [P, 6])
        mv = sb("mv", [P, 2])
        std = sb("std", [P, 1])
        rstd = sb("rstd", [P, 1])

        banks = [ctx.enter_context(nc.psum_tensor(f"bank{i}", [P, BANK], fp32)) for i in range(8)]
        PACK, XT, KV = 0, 2, 4
        XQ_PS, OT_PS, Q_PS, O_PS, Y_PS = 2, 3, 4, 6, 7

        w_in = sem("w_in")
        wq_in = sem("wq_in")
        column_ok = sem("column_ok")
        column_in = sem("column_in")
        adj_used = sem("adj_used")
        kv_copied = sem("kv_copied")
        order_out = sem("order_out")
        order_in = sem("order_in")
        wo_in = sem("wo_in")
        flag_ok = sem("flag_ok")
        sparse_done = sem("sparse_done")
        ident_zero = sem("ident_zero")
        ident_ok = sem("ident_ok")
        before_zero = sem("before_zero")
        sort_consts = sem("sort_consts")
        arena_zero = sem("arena_zero")
        rank_ok = sem("rank_ok")
        near_ok = sem("near_ok")
        joined = sem("joined")
        pv_ps = sem("pv_ps")
        normed = sem("normed")
        digits_ok = sem("digits_ok")
        diag_ok = sem("diag_ok")
        keys_ok = sem("keys_ok")
        packed = sem("packed")
        xT_ps = sem("xT_ps")
        xT_ok = sem("xT_ok")
        kv_ps = sem("kv_ps")
        onehot_ok = sem("onehot_ok")
        place_ps = sem("place_ps")
        xqT_ps = sem("xqT_ps")
        shifted = sem("shifted")
        xqT_ok = sem("xqT_ok")
        q_ps = sem("q_ps")
        weighted = sem("weighted")
        o_copied = sem("o_copied")
        oT_ps = sem("oT_ps")
        oT_copied = sem("oT_copied")
        y_ps = sem("y_ps")
        bad_ok = sem("bad_ok")
        bad_ps = sem("bad_ps")
        eps_ok = sem("eps_ok")
        exps = sem("exps")
        ln_ok = sem("ln_ok")
        rs_ok = sem("rs_ok")
        less_ok = sem("less_ok")
        squares_ok = sem("squares_ok")
        shift_ok = sem("shift_ok")
        base_ok = sem("base_ok")
        decoded = sem("decoded")
        named = sem("named")
        placed = sem("placed")
        mask_ok = sem("mask_ok")
        excess_ok = sem("excess_ok")
        scores = sem("scores")
        products = sem("products")
        masked = sem("masked")
        maxima = sem("maxima")
        sums = sem("sums")
        inverses = sem("inverses")
        probs = sem("probs")
        bad_part = sem("bad_part")
        x_in = [sem(f"x_in{i}") for i in range(4)]
        adj_in = [sem(f"adj_in{i}") for i in range(2)]
        rows_out = [sem(f"rows_out{i}") for i in range(4)]
        kv_in = [sem(f"kv_in{i}") for i in range(RING)]
        xq_in = [sem(f"xq_in{i}") for i in range(RING)]
        given = [sem(f"given{i}") for i in range(RESULTS)]
        passed_sp = sem("passed_sp")
        passed_pe = sem("passed_pe")
        passed_dve = sem("passed_dve")
        g_xT_ok = sem("g_xT_ok")
        g_q_ps = sem("g_q_ps")
        g_res_in = sem("g_res_in")
        g_head_in = sem("g_head_in")
        g_k_in = sem("g_k_in")
        g_kT_ps = sem("g_kT_ps")
        g_kT_ok = sem("g_kT_ok")
        g_q_in = sem("g_q_in")
        g_adj_in = sem("g_adj_in")
        g_qT_ps = sem("g_qT_ps")
        g_qT_ok = sem("g_qT_ok")
        g_diag = sem("g_diag")
        g_bias = sem("g_bias")
        g_s_ps = sem("g_s_ps")
        g_logits = sem("g_logits")
        g_max = sem("g_max")
        g_exp = sem("g_exp")
        g_rinv = sem("g_rinv")
        g_pT_ps = sem("g_pT_ps")
        g_pT_ok = sem("g_pT_ok")
        g_pv = sem("g_pv")
        g_o = sem("g_o")
        g_oT_ps = sem("g_oT_ps")
        g_oT_ok = sem("g_oT_ok")
        g_head_done = sem("g_head_done")
        g_res = sem("g_res")
        g_stats = sem("g_stats")
        g_mv = sem("g_mv")
        g_std = sem("g_std")
        g_rstd = sem("g_rstd")
        g_ln = sem("g_ln")
        g_out = sem("g_out")

        block = ctx.enter_context(nc.Block())

        x_v = x.rearrange("(t p) d -> t p d", p=P)
        adj_t = adj.rearrange("(t p) m -> t p m", p=P)
        kv_v = kv.rearrange("(t p) c -> t p c", p=P)
        order_g = order.rearrange("(g i p) c -> g p i c", i=GT, p=P)
        kv_h = kv.rearrange("(t p) (g k) -> p t g k", p=P, k=KD)
        kv_b = kv.rearrange("(b t p) (g k) -> b p t g k", p=P, t=4, k=KD)
        out_t = out.rearrange("(t p) d -> t p d", p=P)

        def gathered(t):
            return arena[:, ROOM[t][0]:ROOM[t][0] + CAP[t], :]

        def weighings(t):
            return sum(-(-CAP[i] // WEIGHED) for i in range(t))

        def late_tile(v):
            return EARLY + v - LATE_FROM if 0 <= v - LATE_FROM < T - EARLY else None

        def scanned(e):
            return 3 * (e // 4) + e % 4 if e % 4 < 3 else None

        def every_turn(eng, turn, between):
            turn(0, first=True)
            with eng.Fori(1, TURNS - 1) as i:
                turn(i)
            between()
            turn(TURNS - 1, last=True)

        @block.sync
        def _(sp):
            for n in range(2):
                sp.dma_start(row[:, n, 2 * HK:], x_v[n, :, :]).then_inc(x_in[n], 16)
            for c in range(DC):
                for j, wsrc in enumerate((wks, wvs)):
                    sp.dma_start(w[:, c, j * HK:(j + 1) * HK].rearrange("p (h k) -> p h k", h=H),
                                 wsrc[:, c * P:(c + 1) * P, :].rearrange("h p k -> p h k")).then_inc(w_in, 16)
            sp.dma_start(adj_sb[:, 0, :, :].rearrange("p h m -> p (h m)"), adj_t[0, :, :]).then_inc(adj_in[0], 16)
            sp.wait_ge(column_ok, 2)
            sp.dma_start(column[1:2, :], column_lo[0:1, :]).then_inc(column_in, 16)

            def load_adj(t, b, first=False):
                if not first:
                    sp.wait_ge(adj_used, t - 1)
                sp.dma_start(adj_sb[:, b, :, :].rearrange("p h m -> p (h m)"), adj_t[t, :, :]).then_inc(adj_in[b], 16)

            def store(n, b):
                sp.wait_ge(kv_copied, n * 2 + 2)
                sp.sem_inc(passed_sp, 1)
                sp.dma_start(kv_v[n, :, :], row[:, b, 0:2 * HK]).then_inc(rows_out[b], 16)

            def turn(i, first=False, last=False):
                for e in range(TILES):
                    n = i * TILES + e
                    if not (last and e >= TILES - 2):
                        b = (e + 2) % 4
                        if not (first and e < 2):
                            sp.wait_ge(xT_ps, n - 1)
                            sp.sem_inc(passed_sp, 1)
                        sp.dma_start(row[:, b, 2 * HK:], x_v[n + 2, :, :]).then_inc(x_in[b], 16)
                    j = scanned(e)
                    if j is not None:
                        load_adj(i * SCANS + j + 1, (j + 1) % 2, first=(first and j == 0))
                    if not (first and e < 2):
                        store(n - 2, (e - 2) % 4)

            def read_order(g):
                sp.wait_ge(order_out, (g + 1) * (16 * GT))
                sp.dma_start(srt[:, g * GT:(g + 1) * GT, :], order_g[g, :, :, :]).then_inc(order_in, 16)

            def other_weights():
                for c in range(DC):
                    sp.dma_start(w[:, c, 2 * HK:].rearrange("p (h k) -> p h k", h=H),
                                 wqs[:, c * P:(c + 1) * P, :].rearrange("h p k -> p h k")).then_inc(wq_in, 16)
                sp.dma_start(wo_sb[:], wo.rearrange("h k o -> (h k) o").rearrange("(c p) o -> p c o", p=P)).then_inc(wo_in, 16)

            every_turn(sp, turn, other_weights)
            for n in (T - 2, T - 1):
                store(n, n % 4)
            read_order(0)
            for t in range(TURNS * SCANS + 1, T):
                if t == EARLY + 1:
                    sp.wait_ge(kv_in[LATE_FROM], 16 * CAP[LATE_FROM])
                load_adj(t, t % 2)
            read_order(1)

            sp.wait_ge(flag_ok, 1)
            crowded = sp.value_load(flag[0:1, 0:1], min_val=0, max_val=1 << 20)
            sp.wait_ge(sparse_done, 1)
            with sp.If(crowded > 0):
                sp.dma_start(res[:], x.rearrange("(t p) d -> p t d", p=P)).then_inc(g_res_in, 16)
                with sp.Fori(0, H) as h:
                    sp.wait_ge(g_head_done, h * T + 1)
                    sp.dma_start(vh[:], kv_h[:, :, H + h, :]).then_inc(g_head_in, 16)
                    sp.dma_start(woh[:], wo[h, :, :]).then_inc(g_head_in, 16)
                    sp.dma_start(wqh[:], wqs[h, :, :].rearrange("(c p) k -> p c k", p=P)).then_inc(g_head_in, 16)
                    with sp.Fori(0, NB) as b:
                        sp.wait_ge(g_kT_ps, h * NB + b + 1)
                        sp.dma_start(k_nat[:], kv_b[b, :, :, h, :]).then_inc(g_k_in, 16)
                    with sp.Fori(0, T) as t:
                        sp.wait_ge(g_qT_ps, h * T + t + 1)
                        sp.dma_start(x_nat[:], x_v[t, :, :]).then_inc(g_q_in, 16)
                        sp.wait_ge(g_pT_ps, (h * T + t) * NB + 1)
                        sp.dma_start(logits[:], adj_t[t, :, :]).then_inc(g_adj_in, 16)
                with sp.Fori(0, T) as t:
                    sp.wait_ge(g_ln, t + 1)
                    sp.dma_start(out_t[t, :, :], res[:, t, :]).then_inc(g_out, 16)
                sp.wait_ge(g_out, 16 * T)

        @block.gpsimd
        def _(pool):
            nc.gpsimd.memset(ident[:], 0.0).then_inc(ident_zero, 1)
            nc.gpsimd.iota(column[0:1, :], [[256, BANK // 256], [0, 256]], base=0, channel_multiplier=0,
                           allow_small_or_imprecise_dtypes=True).then_inc(column_ok, 1)
            nc.gpsimd.iota(column_lo[:], [[0, BANK // 256], [1, 256]], base=0, channel_multiplier=0,
                           allow_small_or_imprecise_dtypes=True).then_inc(column_ok, 1)
            pool.wait_ge(ident_zero, 1)
            nc.gpsimd.affine_select(out=ident[:], in_=ident[:], compare_op=ALU.not_equal, fill=1.0, base=0,
                                    pattern=[[-1, P]], channel_multiplier=1).then_inc(ident_ok, 1)
            nc.gpsimd.memset(before[:], 0.0).then_inc(before_zero, 1)
            nc.gpsimd.memset(ones[:], 1.0).then_inc(sort_consts, 1)
            nc.gpsimd.iota(degrees[:], [[-1, NEAR], [0, GT]], base=NEAR, channel_multiplier=0,
                           allow_small_or_imprecise_dtypes=True).then_inc(sort_consts, 1)
            nc.gpsimd.iota(nodes[:], [[P, T]], base=0, channel_multiplier=1).then_inc(sort_consts, 1)
            pool.wait_ge(before_zero, 1)
            nc.gpsimd.affine_select(out=before[:], in_=before[:], compare_op=ALU.is_gt, fill=-1.0, base=0,
                                    pattern=[[1, P]], channel_multiplier=-1).then_inc(sort_consts, 1)
            nc.gpsimd.memset(arena[:], 0.0).then_inc(arena_zero, 1)
            pool.wait_ge(arena_zero, 1)

            def write_order(g, part=0, parts=1):
                pool.wait_ge(rank_ok, g + 1)
                for i in range(g * GT + part * GT // parts, g * GT + (part + 1) * GT // parts):
                    nc.gpsimd.indirect_dma_start(order[:, :], bass.IndirectOffsetOnAxis(ap=rank[:, i:i + 1], axis=0),
                                                 rec[:, i, :], None).then_inc(order_out, 16)

            write_order(0)
            for b in range(4):
                pool.wait_ge(rows_out[b], 16 * (T // 4))

            def fetch_x(t):
                place = ORDER[t]
                pool.wait_ge(near_ok, t // GT + 1)
                if t >= RING:
                    pool.wait_ge(y_ps, t - RING + 1)
                nc.gpsimd.indirect_dma_start(xq[:, t % RING, :], None, x[:, :],
                                             bass.IndirectOffsetOnAxis(ap=near[:, place, 0:1], axis=0)).then_inc(xq_in[t % RING], 16)

            def fetch(t):
                place = ORDER[t]
                if ROOM[t][1]:
                    pool.wait_ge(pv_ps, ROOM[t][1])
                for a in range(CAP[t]):
                    nc.gpsimd.indirect_dma_start(gathered(t)[:, a, :], None, kv[:, :],
                                                 bass.IndirectOffsetOnAxis(ap=near[:, place, 1 + a:2 + a], axis=0),
                                                 bounds_check=N - 1, oob_is_err=False).then_inc(kv_in[t % RING], 16)

            def give(t):
                pool.wait_ge(normed, t + 1)
                nc.gpsimd.indirect_dma_start(out[:, :], bass.IndirectOffsetOnAxis(ap=near[:, ORDER[t], 0:1], axis=0),
                                             joined_sb[:, t % RESULTS, :], None).then_inc(given[t % RESULTS], 16)

            for t in range(X_AHEAD):
                fetch_x(t)
            for t in range(T + LAG):
                if t + X_AHEAD < T:
                    fetch_x(t + X_AHEAD)
                if t < T:
                    fetch(t)
                if 0 <= t - ORDER_AT < ORDER_PARTS:
                    write_order(1, t - ORDER_AT, ORDER_PARTS)
                if t >= LAG:
                    give(t - LAG)
            for b in range(RESULTS):
                pool.wait_ge(given[b], 16 * len(range(b, T, RESULTS)))
            pool.sem_inc(sparse_done, 1)

        @block.tensor
        def _(pe):
            pe.wait_ge(ident_ok, 1)
            pe.wait_ge(digits_ok, 2 + DIGITS)
            pe.wait_ge(w_in, 16 * 2 * DC)

            def pack(t, b, first=False):
                pe.wait_ge(diag_ok, t + 1)
                if not first:
                    pe.wait_ge(keys_ok, t - 1)
                packed_ps = banks[PACK + b][:]
                halves = adj_sb[:, b, :, :].rearrange("p h m -> p (h m)").bitcast(bf16).rearrange("p (m two) -> p m two", two=2)
                for k in range(DIGITS):
                    last = nc.tensor.matmul(packed_ps, digit[:, k, :], halves[:, k * BANK:(k + 1) * BANK, 1],
                                            start=(k == 0), stop=False)
                last.then_inc(adj_used, 1)
                nc.tensor.matmul(packed_ps, ones2[:], column[:], start=False, stop=True).then_inc(packed, 1)

            def project(n, b, x_loads, first=False):
                pe.wait_ge(x_in[b], x_loads * 16)
                for c in range(DC):
                    last = nc.tensor.transpose(banks[XT + b % 2][:, c * P:(c + 1) * P],
                                               row[:, b, 2 * HK + c * P:2 * HK + (c + 1) * P], ident[:])
                last.then_inc(xT_ps, 1)
                pe.wait_ge(xT_ok, n + 1)
                for j in range(2):
                    if not first:
                        pe.wait_ge(kv_copied, n * 2 - 3 + j)
                    for c in range(DC):
                        last = nc.tensor.matmul(banks[KV + 2 * (b % 2) + j][:], xT[:, b % 2, c, :],
                                                w[:, c, j * HK:(j + 1) * HK], start=(c == 0), stop=(c == DC - 1))
                    last.then_inc(kv_ps, 1)

            def places(g):
                flat = onehot[:].rearrange("p d t -> p (d t)")
                pe.wait_ge(onehot_ok, g + 1)
                nc.tensor.matmul(banks[PACK][:, 0:NEAR * GT], ones[:], flat, start=True, stop=True)
                nc.tensor.matmul(banks[PACK][:, NEAR * GT:2 * NEAR * GT], before[:], flat, start=True,
                                 stop=True).then_inc(place_ps, 1)

            def turn(i, first=False, last=False):
                for e in range(TILES):
                    project(i * TILES + e, e % 4, i * (TILES // 4) + e // 4 + 1, first=(first and e < 2))
                    if first and e == 0:
                        pe.wait_ge(column_in, 16)
                    j = scanned(e)
                    if j is not None:
                        if last and j == 4:
                            pe.wait_ge(rank_ok, 1)
                        pack(i * SCANS + j, j % 2, first=(first and j < 2))
                    if last and e == 3:
                        pe.wait_ge(keys_ok, i * SCANS + 3)
                        places(0)

            pe.wait_ge(sort_consts, 4)
            every_turn(pe, turn, lambda: None)

            def turned(t):
                pe.wait_ge(xq_in[t % RING], (t // RING + 1) * 16)
                for c in range(DC):
                    last = nc.tensor.transpose(banks[XQ_PS][:, c * P:(c + 1) * P], xq[:, t % RING, c * P:(c + 1) * P], ident[:])
                last.then_inc(xqT_ps, 1)

            def query(t):
                if t >= 2:
                    pe.wait_ge(shifted, t - 1)
                pe.wait_ge(xqT_ok, t + 1)
                for c in range(DC):
                    last = nc.tensor.matmul(banks[Q_PS + t % 2][:], xT[:, 0, c, :], w[:, c, 2 * HK:],
                                            start=(c == 0), stop=(c == DC - 1))
                last.then_inc(q_ps, 1)

            def accumulate(t):
                v = gathered(t)
                done = weighings(t)
                for a in range(CAP[t]):
                    if a % WEIGHED == 0:
                        done += 1
                        pe.wait_ge(weighted, done)
                    last = nc.tensor.matmul(banks[O_PS][:], ident[:], v[:, a, HK:], start=(a == 0), stop=(a == CAP[t] - 1))
                last.then_inc(pv_ps, 1)

            def turn_sum(t):
                pe.wait_ge(o_copied, t + 1)
                for k in range(HC):
                    last = nc.tensor.transpose(banks[OT_PS][:, k * P:(k + 1) * P], o_sb[:, k * P:(k + 1) * P], ident[:])
                last.then_inc(oT_ps, 1)

            def project_sum(t):
                if t:
                    pe.wait_ge(joined, t)
                nc.tensor.matmul(banks[Y_PS][:, 0:D], ident[:], xq[:, t % RING, :], start=True, stop=False)
                pe.wait_ge(oT_copied, t + 1)
                for k in range(HC):
                    last = nc.tensor.matmul(banks[Y_PS][:, 0:D], oT_sb[:, k, :], wo_sb[:, k, :],
                                            start=False, stop=(k == HC - 1))
                last.then_inc(y_ps, 1)

            for t in range(TURNS * SCANS, EARLY):
                pack(t, t % 2)
            pe.wait_ge(wq_in, 16 * DC)
            pe.wait_ge(wo_in, 16)
            pe.wait_ge(kv_copied, 2 * T)
            for t in range(2):
                turned(t)
                query(t)
            turned(2)
            for v in range(T + 1):
                if v == SORT_AT:
                    places(1)
                if v:
                    accumulate(v - 1)
                scanning = late_tile(v) is not None
                if scanning:
                    pack(late_tile(v), late_tile(v) % 2)
                elif v + 2 < T:
                    query(v + 2)
                if v:
                    turn_sum(v - 1)
                if scanning:
                    query(v + 2)
                if v + 3 < T:
                    turned(v + 3)
                if v:
                    project_sum(v - 1)

            pe.wait_ge(bad_ok, 1)
            nc.tensor.matmul(banks[PACK][:, 0:NBAD], ones_f[:, 0:P], bad[:], start=True, stop=True).then_inc(bad_ps, 1)
            pe.wait_ge(flag_ok, 1)
            crowded = pe.value_load(flag[0:1, 0:1], min_val=0, max_val=1 << 20)
            pe.wait_ge(sparse_done, 1)
            with pe.If(crowded > 0):
                for count in (g_head_done, g_kT_ps, g_qT_ps, g_pT_ps, g_pv, g_s_ps):
                    pe.sem_inc(count, 1)
                with pe.Fori(0, H) as h:
                    with pe.Fori(0, NB) as b:
                        pe.wait_ge(g_k_in, (h * NB + b + 1) * 16)
                        pe.wait_ge(g_kT_ok, h * NB + b + 1)
                        pe.sem_inc(passed_pe, 1)
                        for j in range(4):
                            last = nc.tensor.transpose(banks[0][0:KD, j * P:(j + 1) * P], k_nat[:, j, :], ident[:])
                        last.then_inc(g_kT_ps, 1)
                    pe.wait_ge(g_kT_ok, (h + 1) * NB + 1)
                    pe.wait_ge(g_head_in, (h + 1) * 48)
                    pe.sem_inc(passed_pe, 1)
                    with pe.Fori(0, T) as t:
                        n = h * T + t
                        pe.wait_ge(g_q_in, (n + 1) * 16)
                        pe.sem_inc(passed_pe, 1)
                        for c in range(DC):
                            last = nc.tensor.transpose(banks[1][:, c * P:(c + 1) * P], x_nat[:, c * P:(c + 1) * P], ident[:])
                        last.then_inc(g_qT_ps, 1)
                        pe.wait_ge(g_xT_ok, n + 1)
                        pe.sem_inc(passed_pe, 1)
                        for c in range(DC):
                            last = nc.tensor.matmul(banks[0][0:KD, 0:P], wqh[:, c, :], x_natT[:, c, :],
                                                    start=(c == 0), stop=(c == DC - 1))
                        last.then_inc(g_q_ps, 1)
                        pe.wait_ge(g_qT_ok, n + 1)
                        for c in range(NB):
                            if c < 2:
                                pe.wait_ge(g_logits, n * NB + 1)
                            else:
                                pe.wait_ge(g_logits, n * NB + c - 1 + 1)
                            nc.tensor.matmul(banks[2 + c % 2][:], qT[:], kT[:, c * BANK:(c + 1) * BANK],
                                             start=True, stop=True).then_inc(g_s_ps, 1)
                        pe.wait_ge(g_exp, n + 1)
                        pe.wait_ge(g_o, n + 1)
                        for c in range(NB):
                            if c < 2:
                                pe.wait_ge(g_pT_ok, n * NB + 1)
                            else:
                                pe.wait_ge(g_pT_ok, n * NB + c - 1 + 1)
                            for j in range(4):
                                last = nc.tensor.transpose(banks[4 + c % 2][:, j * P:(j + 1) * P],
                                                           logits[:, (4 * c + j) * P:(4 * c + j + 1) * P], ident[:])
                            last.then_inc(g_pT_ps, 1)
                            pe.wait_ge(g_pT_ok, n * NB + c + 1 + 1)
                            for j in range(4):
                                last = nc.tensor.matmul(banks[6][:, 0:KD], pT[:, c % 2, j * P:(j + 1) * P], vh[:, 4 * c + j, :],
                                                        start=(c + j == 0), stop=(c == NB - 1 and j == 3))
                            last.then_inc(g_pv, 1)
                        pe.wait_ge(g_o, n + 1 + 1)
                        pe.sem_inc(passed_pe, 1)
                        nc.tensor.transpose(banks[1][0:KD, 0:P], o_n[:], ident[:]).then_inc(g_oT_ps, 1)
                        pe.wait_ge(g_oT_ok, n + 1)
                        pe.wait_ge(g_res, n + 1)
                        nc.tensor.matmul(banks[7][:, 0:D], oT[:], woh[:], start=True, stop=True).then_inc(g_head_done, 1)

        @block.scalar
        def _(act):
            nc.scalar.preload_act_table_set("natural_log_exp_and_others")

            def turn(i, first=False, last=False):
                for e in range(TILES):
                    n = i * TILES + e
                    act.wait_ge(xT_ps, n + 1)
                    if not (first and e < 2):
                        act.wait_ge(kv_ps, n * 2 - 2)
                    nc.scalar.copy(xT[:, e % 2, :, :],
                                   banks[XT + e % 2][:, 0:D].rearrange("p (c q) -> p c q", c=DC)).then_inc(xT_ok, 1)
                    if not (first and e < 4):
                        act.wait_ge(rows_out[e % 4], i * 32 + (e // 4) * 16)
                    for j in range(2):
                        act.wait_ge(kv_ps, n * 2 + j + 1)
                        nc.scalar.copy(row[:, e % 4, j * HK:(j + 1) * HK], banks[KV + 2 * (e % 2) + j][:]).then_inc(kv_copied, 1)

            every_turn(act, turn, lambda: None)
            act.wait_ge(eps_ok, 1)

            def turned(t):
                act.wait_ge(xqT_ps, t + 1)
                if t == 0:
                    act.wait_ge(kv_ps, 2 * T)
                nc.scalar.copy(xT[:, 0, :, :], banks[XQ_PS][:, 0:D].rearrange("p (c q) -> p c q", c=DC)).then_inc(xqT_ok, 1)

            def weights(t):
                s = t % SIDES
                act.wait_ge(shifted, t + 1)
                nc.scalar.activation(pr[:, s, 0:CAP[t], :], lg[:, s, 0:CAP[t], :], ACT.Exp).then_inc(exps, 1)

            def copies(t):
                act.wait_ge(pv_ps, t + 1)
                nc.scalar.copy(o_sb[:], banks[O_PS][:]).then_inc(o_copied, 1)
                act.wait_ge(oT_ps, t + 1)
                nc.scalar.copy(oT_sb[:].rearrange("p c q -> p (c q)"), banks[OT_PS][:]).then_inc(oT_copied, 1)

            def join(t):
                r = t % RESULTS
                act.wait_ge(y_ps, t + 1)
                if t >= RESULTS:
                    act.wait_ge(given[r], 16 * (t // RESULTS))
                nc.scalar.activation(joined_sb[:, r, :], banks[Y_PS][:, 0:D], ACT.Copy,
                                     accum_out=total[:, t % SIDES, :]).then_inc(joined, 1)

            def norm(t):
                s = t % SIDES
                r = t % RESULTS
                act.wait_ge(joined, t + 1)
                nc.scalar.activation(less[:, s, :], total[:, s, :], ACT.Copy, scale=-1.0 / D).then_inc(less_ok, 1)
                act.wait_ge(less_ok, t + 1)
                nc.scalar.activation(square[:], joined_sb[:, r, :], ACT.Square, bias=less[:, s, 0:1],
                                     accum_out=squares[:, s, :]).then_inc(squares_ok, 1)
                act.wait_ge(squares_ok, t + 1)
                nc.scalar.activation(lnv[:, s, :], squares[:, s, :], ACT.Ln, scale=1.0 / D, bias=eps[:, 0:1]).then_inc(ln_ok, 1)
                act.wait_ge(ln_ok, t + 1)
                nc.scalar.activation(rs4[:, s, :], lnv[:, s, :], ACT.Exp, scale=-0.5).then_inc(rs_ok, 1)
                act.wait_ge(rs_ok, t + 1)
                nc.scalar.activation(shift[:, s, :], less[:, s, :], ACT.Copy, scale=rs4[:, s, 0:1]).then_inc(shift_ok, 1)
                act.wait_ge(shift_ok, t + 1)
                nc.scalar.activation(joined_sb[:, r, :], joined_sb[:, r, :], ACT.Identity, bias=shift[:, s, 0:1],
                                     scale=rs4[:, s, 0:1]).then_inc(normed, 1)

            for t in range(3):
                turned(t)
            for v in range(T + 2):
                if v < T:
                    weights(v)
                if v >= 2:
                    join(v - 2)
                if 1 <= v <= T:
                    copies(v - 1)
                if v + 3 < T:
                    turned(v + 3)
                if v >= 2:
                    norm(v - 2)

            act.wait_ge(flag_ok, 1)
            crowded = act.value_load(flag[0:1, 0:1], min_val=0, max_val=1 << 20)
            act.wait_ge(sparse_done, 1)
            with act.If(crowded > 0):
                for count in (g_kT_ok, g_pT_ok):
                    act.sem_inc(count, 1)
                with act.Fori(0, H) as h:
                    with act.Fori(0, NB) as b:
                        act.wait_ge(g_kT_ps, h * NB + b + 1 + 1)
                        act.wait_ge(g_head_done, h * T + 1)
                        nc.scalar.copy(kT[:, bass.ds(b * BANK, BANK)], banks[0][0:KD, :]).then_inc(g_kT_ok, 1)
                    with act.Fori(0, T) as t:
                        n = h * T + t
                        act.wait_ge(g_qT_ps, n + 1 + 1)
                        nc.scalar.copy(x_natT[:].rearrange("p c q -> p (c q)"), banks[1][:, 0:D]).then_inc(g_xT_ok, 1)
                        act.wait_ge(g_q_ps, n + 1)
                        act.wait_ge(g_s_ps, n * NB + 1)
                        nc.scalar.copy(qT[:], banks[0][0:KD, 0:P]).then_inc(g_qT_ok, 1)
                        act.wait_ge(g_max, n + 1)
                        nc.scalar.activation(logits[:], logits[:], ACT.Exp, bias=nmax[:, 0:1],
                                             accum_out=rsum[:, 0:1]).then_inc(g_exp, 1)
                        for c in range(NB):
                            act.wait_ge(g_pT_ps, n * NB + c + 1 + 1)
                            if c < 2:
                                act.wait_ge(g_pv, n * NB + 1)
                            else:
                                act.wait_ge(g_pv, n * NB + c - 1 + 1)
                            nc.scalar.copy(pT[:, c % 2, :], banks[4 + c % 2][:]).then_inc(g_pT_ok, 1)
                        act.wait_ge(g_oT_ps, n + 1)
                        nc.scalar.copy(oT[:], banks[1][0:KD, 0:P]).then_inc(g_oT_ok, 1)
                act.wait_ge(eps_ok, 1)
                with act.Fori(0, T) as t:
                    act.wait_ge(g_mv, t + 1)
                    nc.scalar.activation(std[:], mv[:, 1:2], ACT.Sqrt, bias=eps[:, 0:1]).then_inc(g_std, 1)

        @block.vector
        def _(dve):
            nc.vector.memset(ones2[:], 1.0).then_inc(digits_ok, 1)
            nc.vector.memset(ones_f[:], 1.0).then_inc(digits_ok, 1)
            nc.vector.memset(eps[:], EPS).then_inc(eps_ok, 1)
            dve.wait_ge(ident_ok, 1)
            for k in range(DIGITS):
                nc.vector.tensor_scalar(digit[:, k, :], ident[:], float(KEY << k), None, ALU.mult).then_inc(digits_ok, 1)

            nc.vector.memset(base[:], 0.0).then_inc(base_ok, 1)
            dve.wait_ge(sort_consts, 4)
            nc.vector.tensor_copy(rec[:, :, 0], nodes[:]).then_inc(named, 1)

            def itself(t, b, loads):
                dve.wait_ge(adj_in[b], loads * 16)
                d = adj_sb[:, b, :, :].rearrange("p h m -> p (h m)")[:, bass.ds(t * P, P)]
                nc.vector.tensor_tensor(d, d, ident[:], ALU.max).then_inc(diag_ok, 1)

            def largest(t, b, j):
                dve.wait_ge(packed, t + 1)
                dve.sem_inc(passed_dve, 1)
                for e in range(SEGS):
                    last = nc.vector.max(keys[:, j, e * 8:(e + 1) * 8], banks[PACK + b][:, e * SEG:(e + 1) * SEG])
                last.then_inc(keys_ok, 1)

            def decode(i, size=BATCH):
                n = [0]
                of = slice(0, size)
                tiles = bass.ds(i * BATCH, size)

                def count(ins):
                    n[0] += 1
                    ins.then_inc(decoded, 1)

                def settle():
                    dve.wait_ge(decoded, i * STEPS + n[0])

                dve.wait_ge(keys_ok, i * BATCH + size)
                count(nc.vector.tensor_scalar(col[:, of], keys[:, of], KEY - 1, None, ALU.bitwise_and))
                count(nc.vector.tensor_scalar(bits[:, of], keys[:, of], KEY.bit_length() - 1, None, ALU.logical_shift_right))
                settle()
                count(nc.vector.tensor_copy(val[:, 0, of, :], bits[:, of]))
                eighth = bits[:, of].rearrange("p t (g e) -> p t g e", e=8)[:, :, :, 7]
                count(nc.vector.tensor_reduce(crowd[:, bass.ds(i, 1)], eighth, AX.XY, ALU.max))
                settle()
                for lv in range(LEVELS):
                    raw = val[:, lv, of, :].bitcast(i32)
                    count(nc.vector.tensor_scalar(power[:, of], raw, 0x7F800000, None, ALU.bitwise_and))
                    count(nc.vector.tensor_scalar(expo[:, of], raw, 23, None, ALU.logical_shift_right))
                    settle()
                    count(nc.vector.scalar_tensor_tensor(out=cand[:, of, lv * SEGS * 8:(lv + 1) * SEGS * 8], in0=expo[:, of],
                                                         scalar=float(KEY), in1=col[:, of], op0=ALU.mult, op1=ALU.add))
                    count(nc.vector.tensor_tensor(val[:, lv + 1, of, :], val[:, lv, of, :], power[:, of].bitcast(fp32),
                                                  ALU.subtract))
                    settle()
                count(nc.vector.tensor_reduce(crowd[:, bass.ds(i + len(BATCHES), 1)], val[:, LEVELS, of, :], AX.XY, ALU.max))
                dve.sem_inc(passed_dve, 1)
                for j in range(size):
                    count(nc.vector.max(top[:, j, 0:8], cand[:, j, :]))
                settle()
                dve.sem_inc(passed_dve, 1)
                for j in range(size):
                    count(nc.vector.match_replace(cand2[:, j, :], top[:, j, 0:8], cand[:, j, :], 0.0))
                settle()
                dve.sem_inc(passed_dve, 1)
                for j in range(size):
                    count(nc.vector.max(top[:, j, 8:16], cand2[:, j, :]))
                settle()
                count(nc.vector.tensor_scalar(rec[:, tiles, 1:], top[:, of], float(-BIAS), None, ALU.add))
                count(nc.vector.tensor_scalar(listed[:, of], top[:, of], float(BIAS), None, ALU.is_ge))
                settle()
                count(nc.vector.tensor_reduce(degree[:, tiles], listed[:, of], AX.X, ALU.add))
                assert n[0] == STEPS - 3 * (BATCH - size)

            def count_degrees(g):
                done = [(i + 1) * STEPS - 3 * (BATCH - size) for i, (a, size) in enumerate(BATCHES) if a < (g + 1) * GT]
                dve.wait_ge(decoded, done[-1])
                nc.vector.tensor_tensor(onehot[:], degree[:, g * GT:(g + 1) * GT].unsqueeze(1).to_broadcast([P, NEAR, GT]),
                                        degrees[:], ALU.is_equal).then_inc(onehot_ok, 1)

            def find_places(g):
                flat = place[:].rearrange("p d t -> p (d t)")
                n = NEAR * GT

                def settled(k):
                    dve.wait_ge(placed, g * 3 + k)

                dve.wait_ge(base_ok, g + 1)
                dve.wait_ge(place_ps, g + 1)
                nc.vector.tensor_tensor_scan(flat, ones_f[:, 0:n], banks[PACK][:, 0:n], base[:, 0:1], ALU.mult,
                                             ALU.add).then_inc(placed, 1)
                settled(1)
                nc.vector.tensor_scalar(base[:], base[:], float(GT * P), None, ALU.add).then_inc(base_ok, 1)
                nc.vector.tensor_tensor(flat, flat, banks[PACK][:, n:2 * n], ALU.add).then_inc(placed, 1)
                settled(2)
                nc.vector.tensor_tensor(flat, flat, onehot[:].rearrange("p d t -> p (d t)"), ALU.mult).then_inc(placed, 1)
                settled(3)
                dve.wait_ge(named, 1)
                with nc.allow_low_precision(reason="whole numbers below N"):
                    nc.vector.tensor_reduce(rank[:, g * GT:(g + 1) * GT], place[:].rearrange("p d t -> p t d"), AX.X,
                                            ALU.add).then_inc(rank_ok, 1)

            def lists(g):
                ts = slice(g * GT, (g + 1) * GT)
                dve.wait_ge(order_in, g * 16 + 16)
                nc.vector.scalar_tensor_tensor(out=near[:, ts, :], in0=srt[:, ts, :], scalar=-1.0, in1=srt[:, ts, :],
                                               op0=ALU.mult, op1=ALU.max).then_inc(near_ok, 1)
                nc.vector.tensor_scalar(mask[:, ts, :], srt[:, ts, 1:], 0.0, -BIG, ALU.is_lt, ALU.mult).then_inc(mask_ok, 1)
                for n, (t0, t1, c) in enumerate(LIMITS):
                    k = g * len(LIMITS) + n
                    nc.vector.tensor_reduce(excess[:, k:k + 1], srt[:, g * GT + t0:g * GT + t1, 1 + c], AX.X,
                                            ALU.max).then_inc(excess_ok, 1)

            def scan(i, j):
                itself(i * SCANS + j + 1, (j + 1) % 2, i * (SCANS // 2) + (j + 1) // 2 + 1)
                largest(i * SCANS + j, j % 2, j % BATCH)

            def turn(i, first=False, last=False):
                for j in range(SCANS):
                    scan(i, j)
                    if j == BATCH - 1:
                        if last:
                            find_places(0)
                        decode(i * (SCANS // BATCH))
                if not last:
                    decode(i * (SCANS // BATCH) + 1)

            itself(0, 0, 1)
            every_turn(dve, turn, lambda: count_degrees(0))
            lists(0)
            decode(TURNS * (SCANS // BATCH) - 1)
            for t in range(TURNS * SCANS, EARLY):
                largest(t, t % 2, t % BATCH)

            def score(t):
                s = t % SIDES
                c = CAP[t]
                k = gathered(t)[:, :, 0:HK]
                q = banks[Q_PS + t % 2][:]
                dve.wait_ge(q_ps, t + 1)
                dve.wait_ge(kv_in[t % RING], 16 * sum(CAP[t % RING:t + 1:RING]))
                done = sum(-(-CAP[i] // PIECE) for i in range(t))
                for a in range(0, c, PIECE):
                    b = min(a + PIECE, c)
                    if done:
                        dve.wait_ge(scores, done)
                    done += 1
                    nc.vector.tensor_tensor(prod[:, 0:b - a, :], k[:, a:b, :], q.unsqueeze(1).to_broadcast([P, b - a, HK]),
                                            ALU.mult).then_inc(products, 1)
                    dve.wait_ge(products, done)
                    nc.vector.tensor_reduce(lg[:, s, a:b, :], prod[:, 0:b - a, :].rearrange("p c (h k) -> p c h k", h=H),
                                            AX.X, ALU.add).then_inc(scores, 1)

            def soften(t):
                if t < T:
                    s = t % SIDES
                    c = CAP[t]
                    l = lg[:, s, 0:c, :]
                    dve.wait_ge(mask_ok, t // GT + 1)
                    dve.wait_ge(scores, sum(-(-CAP[i] // PIECE) for i in range(t + 1)))
                    nc.vector.scalar_tensor_tensor(out=l, in0=l, scalar=SCALE,
                                                   in1=mask[:, ORDER[t], 0:c].unsqueeze(2).to_broadcast([P, c, H]),
                                                   op0=ALU.mult, op1=ALU.add).then_inc(masked, 1)
                if t:
                    s1 = (t - 1) % SIDES
                    c1 = CAP[t - 1]
                    p = pr[:, s1, 0:c1, :]
                    dve.wait_ge(exps, t)
                    nc.vector.tensor_reduce(sm[:, s1, :], p.rearrange("p c h -> p h c"), AX.X, ALU.add).then_inc(sums, 1)
                if t < T:
                    dve.wait_ge(masked, t + 1)
                    nc.vector.tensor_reduce(mx[:, s, :], l.rearrange("p c h -> p h c"), AX.X, ALU.max).then_inc(maxima, 1)
                if t:
                    dve.wait_ge(sums, t)
                    nc.vector.reciprocal(inv[:, s1, :], sm[:, s1, :]).then_inc(inverses, 1)
                if t < T:
                    dve.wait_ge(maxima, t + 1)
                    nc.vector.tensor_tensor(l, l, mx[:, s, :].unsqueeze(1).to_broadcast([P, c, H]),
                                            ALU.subtract).then_inc(shifted, 1)
                if t:
                    dve.wait_ge(inverses, t)
                    nc.vector.tensor_tensor(p, p, inv[:, s1, :].unsqueeze(1).to_broadcast([P, c1, H]),
                                            ALU.mult).then_inc(probs, 1)

            def weigh(t):
                c = CAP[t]
                val4 = gathered(t)[:, :, HK:].rearrange("p c (h k) -> p c h k", h=H)
                dve.wait_ge(probs, t + 1)
                for a in range(0, c, WEIGHED):
                    b = min(a + WEIGHED, c)
                    p = pr[:, t % SIDES, a:b, :].unsqueeze(3).to_broadcast([P, b - a, H, KD])
                    nc.vector.tensor_tensor(val4[:, a:b], val4[:, a:b], p, ALU.mult).then_inc(weighted, 1)

            for v in range(T + 1):
                t = late_tile(v)
                done = late_tile(v - 1)
                if v < T:
                    score(v)
                if v == LISTS_AT:
                    lists(1)
                if t is not None:
                    itself(t, t % 2, t // 2 + 1)
                if v <= T:
                    soften(v)
                if 1 <= v <= T:
                    weigh(v - 1)
                if done is not None:
                    largest(done, done % 2, done % BATCH)
                    if done % BATCH == BATCH - 1 or done == T - 1:
                        decode(done // BATCH, done % BATCH + 1)
                if done == T - 1:
                    count_degrees(1)
                if v == SORT_AT:
                    find_places(1)

            dve.wait_ge(excess_ok, G * len(LIMITS))
            nc.vector.tensor_scalar(bad[:, 0:len(BATCHES)], crowd[:, 0:len(BATCHES)], 1.0, None, ALU.is_ge).then_inc(bad_part, 1)
            nc.vector.tensor_scalar(bad[:, len(BATCHES):2 * len(BATCHES)], crowd[:, len(BATCHES):], 0.0, None,
                                    ALU.is_gt).then_inc(bad_part, 1)
            dve.wait_ge(bad_part, 2)
            nc.vector.tensor_scalar(bad[:, 2 * len(BATCHES):], excess[:], 0.0, None, ALU.is_ge).then_inc(bad_ok, 1)
            dve.wait_ge(bad_ps, 1)
            with nc.allow_low_precision(reason="a count"):
                nc.vector.tensor_reduce(flag[:], banks[PACK][:, 0:NBAD], AX.X, ALU.add).then_inc(flag_ok, 1)

            dve.wait_ge(flag_ok, 1)
            crowded = dve.value_load(flag[0:1, 0:1], min_val=0, max_val=1 << 20)
            dve.wait_ge(sparse_done, 1)
            with dve.If(crowded > 0):
                for count in (g_logits, g_o, g_res):
                    dve.sem_inc(count, 1)
                dve.wait_ge(g_res_in, 16)
                with dve.Fori(0, H) as h:
                    with dve.Fori(0, T) as t:
                        n = h * T + t
                        dve.wait_ge(g_adj_in, (n + 1) * 16)
                        nc.vector.tensor_tensor(logits[:, bass.ds(t * P, P)], logits[:, bass.ds(t * P, P)], ident[:],
                                                ALU.max).then_inc(g_diag, 1)
                        dve.wait_ge(g_diag, n + 1)
                        nc.vector.tensor_scalar(logits[:], logits[:], -1.0, BIG, ALU.add, ALU.mult).then_inc(g_bias, 1)
                        dve.wait_ge(g_bias, n + 1)
                        for c in range(NB):
                            dve.wait_ge(g_s_ps, n * NB + c + 1 + 1)
                            piece = logits[:, c * BANK:(c + 1) * BANK]
                            nc.vector.scalar_tensor_tensor(out=piece, in0=banks[2 + c % 2][:], scalar=SCALE, in1=piece,
                                                           op0=ALU.mult, op1=ALU.add).then_inc(g_logits, 1)
                        dve.wait_ge(g_logits, (n + 1) * NB + 1)
                        nc.vector.tensor_reduce(nmax[:], logits[:], AX.X, ALU.max, negate=True).then_inc(g_max, 1)
                        dve.wait_ge(g_exp, n + 1)
                        nc.vector.reciprocal(rinv[:], rsum[:]).then_inc(g_rinv, 1)
                        dve.wait_ge(g_rinv, n + 1)
                        dve.wait_ge(g_pv, (n + 1) * NB + 1)
                        nc.vector.tensor_scalar(o_n[:], banks[6][:, 0:KD], rinv[:, 0:1], None, ALU.mult).then_inc(g_o, 1)
                        dve.wait_ge(g_head_done, n + 1 + 1)
                        r = res[:, bass.ds(t, 1), :].rearrange("p a d -> p (a d)")
                        nc.vector.tensor_tensor(r, r, banks[7][:, 0:D], ALU.add).then_inc(g_res, 1)
                dve.wait_ge(g_res, H * T + 1)
                with dve.Fori(0, T) as t:
                    r = res[:, bass.ds(t, 1), :].rearrange("p a d -> p (a d)")
                    nc.vector.bn_stats(stats[:], r).then_inc(g_stats, 1)
                    dve.wait_ge(g_stats, t + 1)
                    dve.sem_inc(passed_dve, 1)
                    nc.vector.bn_aggr(mv[:], stats[:]).then_inc(g_mv, 1)
                    dve.wait_ge(g_std, t + 1)
                    nc.vector.reciprocal(rstd[:], std[:]).then_inc(g_rstd, 1)
                    dve.wait_ge(g_rstd, t + 1)
                    dve.wait_ge(g_mv, t + 1)
                    nc.vector.tensor_scalar(r, r, mv[:, 0:1], rstd[:, 0:1], ALU.subtract, ALU.mult).then_inc(g_ln, 1)


_INS = ['x', 'adj', 'L0_gnn_Wks', 'L0_gnn_Wqs', 'L0_gnn_Wvs', 'L0_gnn_Wo']


def kernel(**inputs):
    import numpy as _np
    import concourse.bacc as _bacc
    from concourse import mybir as _mybir
    from concourse.bass_utils import run_bass_kernel_spmd as _run

    nc = _bacc.Bacc("TRN2", target_bir_lowering=False, num_devices=1)
    arrays, args = {}, []
    for name in _INS:
        a = _np.ascontiguousarray(inputs[name])
        arrays[f"in_{name}_dram"] = a
        args.append(nc.dram_tensor(f"in_{name}_dram", a.shape, _mybir.dt.from_np(a.dtype), kind="ExternalInput").ap())
    shape = inputs['x'].shape
    args.append(nc.dram_tensor("out_0_dram", shape, _mybir.dt.float32, kind="ExternalOutput").ap())
    graph_attention_resnorm_kernel(nc, *args)
    r = _run(nc, [arrays], core_ids=[0])
    return r.results[0]["out_0_dram"]
```
